# Optimizing a Trainium2 kernel written in Bass

```python
import numpy as np
import jax
import jax.numpy as jnp

def _softmax(x, axis=-1):
    return jax.nn.softmax(x, axis=axis)
def _gelu(x):
    return jax.nn.gelu(x, approximate=True)
def _silu(x):
    return jax.nn.silu(x)
def _sigmoid(x):
    return jax.nn.sigmoid(x)
def _layernorm(x, axis=-1, eps=1e-5):
    m = jnp.mean(x, axis=axis, keepdims=True)
    v = jnp.var(x, axis=axis, keepdims=True)
    return (x - m) / jnp.sqrt(v + eps)
def _scatter_add(tgt, idx, src, axis=0):
    return tgt.at[idx].add(src)
def _segment_sum(src, seg, n):
    return jax.ops.segment_sum(src, seg, n)

kernel_name = 'mk_conv_seq_d2_conv_nchw256_398648'

def setup_inputs(seed: int = 0):
    np.random.seed(seed)
    _w = jnp.asarray
    def _rec_inputs():
        import jax
        import jax.numpy as jnp
        _gk = jax.random.key(seed)
        x = -0.0002928 + 1 * jax.random.normal(jax.random.fold_in(_gk, 1), (16, 256, 32, 32), jnp.float32)
        return x
    x = _rec_inputs()
    def _L0_conv_setup():
        import jax, jax.numpy as jnp
        import numpy as np
        NUM_CH = 256
        NUM_HEAD = 4
        D_K = 64
        key = jax.random.key(seed)
        k1, k2, k3, k4, k5 = jax.random.split(key, 5)
        B, C, H, W = (16, NUM_CH, 32, 32)
        proj_out = NUM_HEAD * D_K * 3
        s_in = 1.0 / np.sqrt(C)
        s_hd = 1.0 / np.sqrt(NUM_HEAD * D_K)
        return {'x': jax.random.normal(k1, (B, C, H, W), dtype=jnp.float32), 'Wp': jax.random.uniform(k2, (proj_out, C), jnp.float32, -s_in, s_in), 'bp': jax.random.uniform(k3, (proj_out,), jnp.float32, -s_in, s_in), 'Wo': jax.random.uniform(k4, (C, NUM_HEAD * D_K), jnp.float32, -s_hd, s_hd), 'bo': jax.random.uniform(k5, (C,), jnp.float32, -s_hd, s_hd)}
    _L0_conv_all = _L0_conv_setup()
    _L0_conv_in = {k: v for k, v in _L0_conv_all.items() if k in ('Wp', 'bp', 'Wo', 'bo', )}
    del _L0_conv_all

    def _L1_conv_setup():
        import jax, jax.numpy as jnp
        import numpy as np
        EPS = 1e-05
        GROUPS = 8

        def group_norm(x, w, b):
            B, C, H, W = x.shape
            xg = x.reshape(B, GROUPS, C // GROUPS, H, W)
            mu = xg.mean(axis=(2, 3, 4), keepdims=True)
            var = xg.var(axis=(2, 3, 4), keepdims=True)
            xn = ((xg - mu) * jax.lax.rsqrt(var + EPS)).reshape(B, C, H, W)
            return xn * w[None, :, None, None] + b[None, :, None, None]
        key = jax.random.key(seed)
        ks = jax.random.split(key, 6)
        B, C, H, W = (32, 256, 32, 32)
        x = jax.random.normal(ks[0], (B, C, H, W), dtype=jnp.float32)
        norm_w = jnp.ones((C,), dtype=jnp.float32)
        norm_b = jnp.zeros((C,), dtype=jnp.float32)
        qkv_w = jax.random.normal(ks[1], (3 * C, C), dtype=jnp.float32) * C ** (-0.5)
        proj_w = jax.random.normal(ks[2], (C, C), dtype=jnp.float32) * C ** (-0.5)
        proj_b = jnp.zeros((C,), dtype=jnp.float32)
        return {'x': x, 'norm_w': norm_w, 'norm_b': norm_b, 'qkv_w': qkv_w, 'proj_w': proj_w, 'proj_b': proj_b}
    _L1_conv_all = _L1_conv_setup()
    _L1_conv_in = {k: v for k, v in _L1_conv_all.items() if k in ('norm_w', 'norm_b', 'qkv_w', 'proj_w', 'proj_b', )}
    del _L1_conv_all

    return {
        "x": x,
        "L0_conv_Wp": _L0_conv_in["Wp"],
        "L0_conv_bp": _L0_conv_in["bp"],
        "L0_conv_Wo": _L0_conv_in["Wo"],
        "L0_conv_bo": _L0_conv_in["bo"],
        "L1_conv_norm_w": _L1_conv_in["norm_w"],
        "L1_conv_norm_b": _L1_conv_in["norm_b"],
        "L1_conv_qkv_w": _L1_conv_in["qkv_w"],
        "L1_conv_proj_w": _L1_conv_in["proj_w"],
        "L1_conv_proj_b": _L1_conv_in["proj_b"],
    }

def reference(x, L0_conv_Wp, L0_conv_bp, L0_conv_Wo, L0_conv_bo, L1_conv_norm_w, L1_conv_norm_b, L1_conv_qkv_w, L1_conv_proj_w, L1_conv_proj_b):
    import jax
    import jax.numpy as jnp
    def _L0_conv_ref(x, Wp, bp, Wo, bo):
        import jax, jax.numpy as jnp
        import numpy as np
        NUM_CH = 256
        NUM_HEAD = 4
        D_K = 64
        B, C, H, W = x.shape
        scale = D_K ** (-0.5)
        xt = x.reshape(B, C, H * W).transpose(0, 2, 1)
        qkv = xt @ Wp.T + bp
        qkv = qkv.reshape(B, -1, NUM_HEAD, 3 * D_K)
        q, k, v = jnp.split(qkv, 3, axis=-1)
        attn = jnp.einsum('bihd,bjhd->bijh', q, k) * scale
        attn = jax.nn.softmax(attn, axis=2)
        res = jnp.einsum('bijh,bjhd->bihd', attn, v)
        res = res.reshape(B, -1, NUM_HEAD * D_K)
        res = res @ Wo.T + bo
        res = res + xt
        return res.transpose(0, 2, 1).reshape(B, C, H, W)

    def _L1_conv_ref(x, norm_w, norm_b, qkv_w, proj_w, proj_b):
        import jax, jax.numpy as jnp
        import numpy as np
        EPS = 1e-05
        GROUPS = 8

        def group_norm(x, w, b):
            B, C, H, W = x.shape
            xg = x.reshape(B, GROUPS, C // GROUPS, H, W)
            mu = xg.mean(axis=(2, 3, 4), keepdims=True)
            var = xg.var(axis=(2, 3, 4), keepdims=True)
            xn = ((xg - mu) * jax.lax.rsqrt(var + EPS)).reshape(B, C, H, W)
            return xn * w[None, :, None, None] + b[None, :, None, None]
        B, C, H, W = x.shape
        N = H * W
        h = group_norm(x, norm_w, norm_b)
        qkv = jnp.einsum('oc,bchw->bohw', qkv_w, h)
        q, k, v = jnp.split(qkv, 3, axis=1)
        q = q.reshape(B, C, N).transpose(0, 2, 1)
        k = k.reshape(B, C, N)
        v = v.reshape(B, C, N).transpose(0, 2, 1)
        attn = jnp.einsum('bnc,bcm->bnm', q, k) * C ** (-0.5)
        attn = jax.nn.softmax(attn, axis=-1)
        out = jnp.einsum('bnm,bmc->bnc', attn, v)
        out = out.transpose(0, 2, 1).reshape(B, C, H, W)
        proj = jnp.einsum('oc,bchw->bohw', proj_w, out) + proj_b[None, :, None, None]
        return x + proj

    def _gn(v, G=32, eps=1e-5):
        B_, C_, H_, W_ = v.shape
        g = v.reshape(B_, G, C_ // G, H_, W_)
        m = jnp.mean(g, axis=(2, 3, 4), keepdims=True)
        s = jnp.var(g, axis=(2, 3, 4), keepdims=True)
        return ((g - m) / jnp.sqrt(s + eps)).reshape(v.shape)

    def _ln_c(v, eps=1e-6):
        m = jnp.mean(v, axis=1, keepdims=True)
        s = jnp.var(v, axis=1, keepdims=True)
        return (v - m) / jnp.sqrt(s + eps)

    def _ln_t(v, eps=1e-5):
        m = jnp.mean(v, axis=-1, keepdims=True)
        s = jnp.var(v, axis=-1, keepdims=True)
        return (v - m) / jnp.sqrt(s + eps)

    def _to_tokens(v):
        B_, C_, H_, W_ = v.shape
        return v.reshape(B_, C_, H_ * W_).transpose(0, 2, 1)
    def _from_tokens(t, like):
        B_, C_, H_, W_ = like.shape
        return t.transpose(0, 2, 1).reshape(B_, C_, H_, W_)

    x = _L0_conv_ref(x, L0_conv_Wp, L0_conv_bp, L0_conv_Wo, L0_conv_bo)
    x = _L1_conv_ref(x, L1_conv_norm_w, L1_conv_norm_b, L1_conv_qkv_w, L1_conv_proj_w, L1_conv_proj_b)
    return x


_drawn_inputs = setup_inputs


def setup_inputs(seed=0):
    import zlib

    import numpy as np

    out = dict(_drawn_inputs(seed))
    spreads = {'L1_conv_norm_w': (1.0, 0.2), 'L1_conv_norm_b': (0.0, 0.1), 'L1_conv_proj_b': (0.0, 0.1)}
    factors = {'L0_conv_Wp': 3.265}
    for name, (base, spread) in spreads.items():
        noise = np.random.default_rng([zlib.crc32(name.encode()), seed]).standard_normal(out[name].shape)
        drawn = base * np.exp(spread * noise) if base else spread * noise
        out[name] = jnp.asarray(drawn.astype(out[name].dtype))
    for name, factor in factors.items():
        out[name] = (out[name] * factor).astype(out[name].dtype)
    return out
```

```python
import numpy as np
import concourse.bass as bass
import concourse.mybir as mybir
from contextlib import ExitStack

F32 = mybir.dt.float32
F32R = mybir.dt.float32r
ALU = mybir.AluOpType
ACT = mybir.ActivationFunctionType
AX = mybir.AxisListType

P = 128
B, C, HW = 16, 256, 32 * 32
HEADS, D = 4, 64
CC = C // P
JT = HW // P
HALF = 512
IT = HALF // P
GROUPS = 8
GSIZE = C // GROUPS
EPS = 1e-5
Q_SCALE = D ** -0.5
L1_SCALE = C ** -0.5
LEAD = 6
LAG = 2
POOL_NORM = (0, 1, 2)

PRO, BODY, LAST = "prologue", "body", "last"
LOOPS = B - 1



def heads(*hs):
    return [("H", h, c) for h in hs for c in range(2)]


L1_UNITS = [("L", 0, 0), ("L", 0, 1)]
NEXT_TILES = [(("H", 2, i // IT), i % IT) for i in range(LEAD)]


def tiles_of(units, gen):
    return [(u, it, gen) for u in units for it in range(IT)]


def make_slots(kind):
    if kind == PRO:
        lead_in, units, gap = 12 + LEAD, heads(0, 1), None
        fill = {0: "w0", 1: "w1", 2: "w2", 3: "w3", 4: "w4", 5: "w5",
                6: "Q0", 7: "K0", 8: "Va", 9: "Vb", 10: "Q1", 11: "K1"}
        do = {2: ["x0"], 4: ["x1"], 13: ["VS"]}
    elif kind == BODY:
        lead_in, units, gap = 0, heads(2, 3, 0, 1) + L1_UNITS, None
        fill = {5: "Q0", 6: "K0", 10: "Va", 11: "Vb", 12: "Q1", 13: "K1", 19: "W0", 20: "W1",
                21: "G1", 22: "G2", 25: "g0", 26: "g1", 28: "va", 29: "vb"}
        do = {0: ["x0"], 3: ["x1"], 8: ["O0"], 17: ["O1", "VS"], 19: ["s0"], 20: ["s1"],
              22: ["h0"], 23: ["h1"]}
    else:
        lead_in, units, gap = 0, heads(2, 3) + L1_UNITS, (16, 15)
        fill = {18: "W0", 19: "W1", 20: "G1", 21: "G2", 22: "g0", 23: "g1", 24: "va", 26: "vb"}
        do = {8: ["O0"], 17: ["O1"], 18: ["s0"], 19: ["s1"], 21: ["h0", "h1"]}
    real = tiles_of(units, 0)
    order = [None] * lead_in + real
    if gap:
        order = order[:gap[0]] + [None] * gap[1] + order[gap[0]:]
    following = [] if kind == LAST else [(u, it, 1) for u, it in NEXT_TILES]
    slots = []
    for s, t in enumerate(order):
        a = s + LEAD
        ahead = order[a] if a < len(order) else (following[a - len(order)] if a - len(order) < len(following) else None)
        slots.append(dict(tile=t, score=ahead, fill=fill.get(s), do=do.get(s, [])))
    return slots


SLOTS = {k: make_slots(k) for k in (PRO, BODY, LAST)}


def value_slots(slots, s):
    out = [s - LAG] if s >= LAG and slots[s - LAG]["tile"] else []
    if s == len(slots) - 1:
        out += [k for k in range(s - LAG + 1, s + 1) if slots[k]["tile"]]
    return out


def finished(slots, s):
    return [slots[k]["tile"][0] for k in value_slots(slots, s) if slots[k]["tile"][1] == IT - 1]




def ring_order(kind):
    out = []
    for sl in SLOTS[kind]:
        out += [sl["fill"]] if sl["fill"] else []
        out += [sl["score"]] if sl["score"] else []
    return out


def softmax_tile(kind, s):
    if s == 0:
        return None if kind == PRO else (*NEXT_TILES[-1], 0)
    return SLOTS[kind][s - 1]["score"]


def norm_tile(kind, s):
    if s == 0:
        return None if kind == PRO else (*NEXT_TILES[-2], 0)
    return softmax_tile(kind, s - 1)


def softmax_order(kind):
    return [t for t in (softmax_tile(kind, s) for s in range(len(SLOTS[kind]))) if t]


def norm_order(kind):
    return [t for t in (norm_tile(kind, s) for s in range(len(SLOTS[kind]))) if t]


def per_slot(kind, of):
    return [x for s in range(len(SLOTS[kind])) for x in of(SLOTS[kind], s)]


def jts(slots, k):
    u, it, _ = slots[k]["tile"]
    return [(u, 2 * it), (u, 2 * it + 1)]


def order_of(pick):
    return {k: pick(k) for k in (PRO, BODY, LAST)}


def done_fills(kind, skip=()):
    return [sl["fill"] for sl in SLOTS[kind] if sl["fill"] and sl["fill"] not in skip]


def tasks(kind, names):
    return [d for sl in SLOTS[kind] for d in sl["do"] if d in names]


NO_HI = ("W0", "W1", "G1", "G2")

ORDER = {
    "ring_full": order_of(ring_order),
    "t_full": order_of(lambda k: per_slot(k, lambda sl, s: jts(sl, s) if sl[s]["tile"] else [])),
    "pv_done": order_of(lambda k: per_slot(k, lambda sl, s: [j for v in value_slots(sl, s) for j in jts(sl, v)])),
    "max_done": order_of(softmax_order),
    "exp_done": order_of(softmax_order),
    "rden_done": order_of(norm_order),
    "norm_act": order_of(lambda k: [t for t in norm_order(k) if t[1] not in POOL_NORM]),
    "norm_pool": order_of(lambda k: [t for t in norm_order(k) if t[1] in POOL_NORM]),
    "hi_done": order_of(lambda k: done_fills(k, NO_HI)),
    "lo_done": order_of(done_fills),
    "acc_lower": order_of(lambda k: [u for u in per_slot(k, finished) if u[0] == "H"]),
    "acc_done": order_of(lambda k: per_slot(k, finished)),
    "split_hi": order_of(lambda k: tasks(k, ("x0", "x1", "VS", "O0", "O1", "h0", "h1"))),
    "split_lo": order_of(lambda k: tasks(k, ("x0", "x1", "O0", "O1", "h0", "h1"))),
    "v3_lo": order_of(lambda k: tasks(k, ("VS",))),
    "h_done": order_of(lambda k: tasks(k, ("h0", "h1"))),
    "stats_done": order_of(lambda k: tasks(k, ("s0", "s1"))),
    "dev_done": order_of(lambda k: ["dev"] if k != PRO else []),
    "rstd_done": order_of(lambda k: ["rstd"] if k != PRO else []),
}
assert len(ORDER["ring_full"][BODY]) % 2 == 0


class At:

    def __init__(self, kind, n):
        self.kind, self.n = kind, n

    def base(self, name):
        o = ORDER[name]
        if self.kind == PRO:
            return 0
        if self.kind == BODY:
            return self.n * len(o[BODY]) + len(o[PRO])
        return LOOPS * len(o[BODY]) + len(o[PRO])

    def back(self, name, key):
        before = [BODY] if self.kind == LAST else [PRO, BODY]
        found = {len(ORDER[name][k]) - ORDER[name][k].index(key) - 1 for k in before}
        assert len(found) == 1, (name, key, found)
        return found.pop()

    def of(self, name, key, previous=False):
        if previous:
            return self.base(name) - self.back(name, key)
        return self.base(name) + ORDER[name][self.kind].index(key) + 1

    def of_tile(self, name, tile):
        if tile in ORDER[name][self.kind]:
            return self.of(name, tile)
        return self.of(name, (tile[0], tile[1], 1), previous=True)

    def ring_buffer(self, key):
        first = 0 if self.kind == PRO else len(ORDER["ring_full"][PRO])
        return (first + ORDER["ring_full"][self.kind].index(key)) % 2


def build_program(nc, x, Wp, bp, Wo, bo, norm_w, norm_b, qkv_w, proj_w, proj_b, out):
    x_t = x.rearrange("b (cc p) h w -> b cc p (h w)", p=P)
    out_t = out.rearrange("b (cc p) h w -> b cc p (h w)", p=P)

    ctx = ExitStack()
    with ctx:
        def sb(name, shape, dt=F32):
            return ctx.enter_context(nc.sbuf_tensor(name, shape, dt))

        def sem(name):
            return ctx.enter_context(nc.semaphore(name))

        x_stage = sb("x_stage", [P, HW])
        resid = sb("resid", [P, CC, HW])
        chan_hi = sb("chan_hi", [P, CC, HW], F32R)
        chan_lo = sb("chan_lo", [P, CC, HW], F32R)
        q_st = sb("q_st", [P, HEADS, HW], F32R)
        k_hh = sb("k_hh", [P, HEADS, HW], F32R)
        k_ll = sb("k_ll", [P, HEADS, HW], F32R)
        v_st = sb("v_st", [P, HEADS, JT, 2 * D], F32R)
        probs = sb("probs", [P, 2 * IT, HW])
        pt_hi = sb("pt_hi", [P, 4, HALF], F32R)
        pt_lo = sb("pt_lo", [P, 4, HALF], F32R)
        o_f = sb("o_f", [P, CC, HW])
        og_hi = sb("og_hi", [P, CC, HW], F32R)
        og_lo = sb("og_lo", [P, CC, HW], F32R)
        v1_hi = sb("v1_hi", [P, JT, C], F32R)
        v1_lo = sb("v1_lo", [P, JT, C], F32R)
        wp_hi = sb("wp_hi", [P, CC, 3, C], F32R)
        wp_lo = sb("wp_lo", [P, CC, 3, C], F32R)
        wo_hi = sb("wo_hi", [P, CC, C], F32R)
        wo_lo = sb("wo_lo", [P, CC, C], F32R)
        a_hi = sb("a_hi", [P, CC, C], F32R)
        a_lo = sb("a_lo", [P, CC, C], F32R)
        b_hi = sb("b_hi", [P, CC, C], F32R)
        b_lo = sb("b_lo", [P, CC, C], F32R)
        bias0 = sb("bias0", [P, 3, CC])
        vecs = sb("vecs", [P, 4, CC])
        ident = sb("ident", [P, P])
        gmean = sb("gmean", [P, P])
        negmax = sb("negmax", [P, 2 * IT])
        den = sb("den", [P, 2 * IT])
        rden = sb("rden", [P, 2 * IT])
        bst = sb("bst", [P, CC, 2, 6])
        mv = sb("mv", [P, CC, 2])
        gm = sb("gm", [P, CC])
        dev = sb("dev", [P, CC])
        dev2 = sb("dev2", [P, CC])
        spread = sb("spread", [P, CC])
        varp = sb("varp", [P, CC])
        mhalf = sb("mhalf", [P, CC])
        rstd = sb("rstd", [P, CC])
        ga = sb("ga", [P, CC])
        gam = sb("gam", [P, CC])
        gb = sb("gb", [P, CC])
        raw_wp = probs[:, 0:2, :].rearrange("p a (b c) -> p (a b) c", c=C)
        raw_wo = probs[:, 2, 0:2 * C].rearrange("p (a c) -> p a c", c=C)
        raw_pj = probs[:, 2, 2 * C:4 * C].rearrange("p (a c) -> p a c", c=C)
        raw_l1 = probs[:, 3:5, :].rearrange("p a (b c) -> p (a b) c", c=C)
        pj_t = probs[:, 5, 0:2 * C].rearrange("p (a c) -> p a c", c=C)

        ring = [ctx.enter_context(nc.psum_tensor(f"ring{i}", [P, HW], F32)) for i in range(2)]
        tbank = [ctx.enter_context(nc.psum_tensor(f"tbank{i}", [P, HALF], F32)) for i in range(2)]
        acc = [ctx.enter_context(nc.psum_tensor(f"acc{i}", [P, HALF], F32)) for i in range(2)]

        S = {name: sem(name) for name in ORDER}
        ring_full, t_full, pv_done = S["ring_full"], S["t_full"], S["pv_done"]
        max_done, exp_done, rden_done = S["max_done"], S["exp_done"], S["rden_done"]
        norm_act, norm_pool = S["norm_act"], S["norm_pool"]
        hi_done, lo_done, acc_lower, acc_done = S["hi_done"], S["lo_done"], S["acc_lower"], S["acc_done"]
        split_hi, split_lo, v3_lo, h_done = S["split_hi"], S["split_lo"], S["v3_lo"], S["h_done"]
        stats_done, dev_done, rstd_done = S["stats_done"], S["dev_done"], S["rstd_done"]
        thi_done, tlo_done = sem("thi_done"), sem("tlo_done")
        chain = sem("chain")
        x_loaded, resid_loaded = sem("x_loaded"), sem("resid_loaded")
        k_dup = [sem("k_dup0"), sem("k_dup1")]
        stored = sem("stored")
        w_loaded, vec_loaded, const_made, bias_scaled = sem("w_loaded"), sem("vec_loaded"), sem("const_made"), sem("bias_scaled")
        CHAIN = 5

        block = ctx.enter_context(nc.Block())

        def buf(unit, it):
            return unit[2] * IT + it

        def image_passes(kind, n):
            return 0 if kind == PRO else n if kind == BODY else LOOPS

        def x_loads(kind, n, cc):
            first = 0 if kind == PRO else 2 * (n + 1)
            return 16 * (first + cc + 1)

        def projections(kind, n):
            return 1 if kind == PRO else n + 2

        def sp_part(sp, kind, n):
            at = At(kind, n)

            def load_x(image, cc):
                sp.dma_start(x_stage[:, :], x_t[image, cc]).then_inc(x_loaded, 16)

            def duplicate_k(pair):
                sp.wait_ge(lo_done, at.of("lo_done", f"K{pair}"))
                for hh in range(2):
                    h, src, dst = 2 * pair + hh, slice(D * hh, D * hh + D), slice(D - D * hh, 2 * D - D * hh)
                    sp.dma_start(k_hh[dst, h, :].bitcast(F32), k_hh[src, h, :].bitcast(F32)).then_inc(k_dup[pair], 16)
                    sp.dma_start(k_ll[dst, h, :].bitcast(F32), k_ll[src, h, :].bitcast(F32)).then_inc(k_dup[pair], 16)

            if kind == PRO:
                load_x(0, 0)
                wp_v = Wp.rearrange("(h t d) c -> t h d c", h=HEADS, t=3)
                for t in range(3):
                    for h in range(HEADS):
                        sp.dma_start(raw_wp[D * (h % 2):D * (h % 2) + D, 2 * t + h // 2, :],
                                     wp_v[t, h]).then_inc(w_loaded, 16)
                sp.dma_start(raw_wo, Wo.rearrange("(a p) c -> p a c", p=P)).then_inc(w_loaded, 16)
                sp.dma_start(raw_pj, proj_w.rearrange("(a p) c -> p a c", p=P)).then_inc(w_loaded, 16)
                sp.dma_start(raw_l1[:, 0:6, :], qkv_w.rearrange("(a p) c -> p a c", p=P)).then_inc(w_loaded, 16)
                bp_v = bp.rearrange("(pr hh t d) -> hh d t pr", pr=2, hh=2, t=3)
                for hh in range(2):
                    for t in range(3):
                        sp.dma_start(bias0[D * hh:D * hh + D, t, :], bp_v[hh, :, t],
                                     allow_slow_non_contiguous=True).then_inc(vec_loaded, 16)
                for i, v in enumerate((bo, norm_w, norm_b, proj_b)):
                    sp.dma_start(vecs[:, i, :], v.rearrange("(a p) -> p a", p=P),
                                 allow_slow_non_contiguous=True).then_inc(vec_loaded, 16)
            if kind == BODY:
                sp.wait_ge(split_lo, at.base("split_lo"))
                load_x(n + 1, 0)
            if kind != LAST:
                sp.wait_ge(split_lo, at.of("split_lo", "x0"))
                load_x(0 if kind == PRO else n + 1, 1)
                duplicate_k(0)
                duplicate_k(1)
            if kind == PRO:
                sp.wait_ge(v3_lo, 1)
            if kind != PRO:
                image = n if kind == BODY else B - 1
                for u in L1_UNITS:
                    sp.wait_ge(acc_done, at.of("acc_done", u))
                    cols = slice(u[2] * HALF, u[2] * HALF + HALF)
                    for cc in range(CC):
                        sp.dma_start(out_t[image, cc, :, cols], resid[:, cc, cols]).then_inc(stored, 16)
            if kind == LAST:
                sp.wait_ge(stored, B * 4 * 16)
            else:
                if kind == BODY:
                    sp.wait_ge(stored, (n + 1) * 4 * 16)
                for cc in range(CC):
                    sp.dma_start(resid[:, cc, :], x_t[0 if kind == PRO else n + 1, cc]).then_inc(resid_loaded, 16)

        def pe_part(pe, kind, n):
            at = At(kind, n)
            slots = SLOTS[kind]
            ring_keys = ORDER["ring_full"][kind]

            def products(dst, terms, start=True, stop=True):
                for i, (lhs, rhs) in enumerate(terms):
                    last = nc.tensor.matmul(dst, lhs, rhs, start=start and i == 0,
                                            stop=stop and i == len(terms) - 1)
                return last

            def take_ring(key):
                i = ring_keys.index(key)
                if i >= 2:
                    old, previous = ring_keys[i - 2], False
                elif kind == PRO:
                    return ring[at.ring_buffer(key)]
                else:
                    old, previous = ORDER["ring_full"][BODY][i - 2], True
                if isinstance(old, str):
                    pe.wait_ge(lo_done, at.of("lo_done", old))
                elif previous and old[:2] == NEXT_TILES[-1]:
                    pe.wait_ge(exp_done, at.of("exp_done", (*old[:2], 0)))
                else:
                    pe.wait_ge(exp_done, at.of("exp_done", old, previous))
                return ring[at.ring_buffer(key)]

            def scores(tile):
                (layer, h, c), it, gen = tile
                dst = take_ring(tile)
                q = slice((c * IT + it) * P, (c * IT + it + 1) * P)
                if layer == "H":
                    if c == 0 and it == 0 and h % 2 == 0:
                        pe.wait_ge(lo_done, at.of("lo_done", f"K{h // 2}"))
                        pe.wait_ge(k_dup[h // 2], projections(kind, n) * 4 * 16)
                    for j in range(2):
                        keys = slice(j * HALF, (j + 1) * HALF)
                        last = products(dst[:, keys], [(q_st[:, h, q], k_hh[:, h, keys]),
                                                       (q_st[:, h, q], k_ll[:, h, keys])])
                else:
                    if c == 0 and it == 0:
                        pe.wait_ge(lo_done, at.of("lo_done", "g1"))
                    for j in range(2):
                        keys = slice(j * HALF, (j + 1) * HALF)
                        last = products(dst[:, keys], [
                            (l[:, cc, q], r[:, cc, keys]) for cc in range(CC)
                            for l, r in ((og_hi, chan_hi), (og_hi, chan_lo), (og_lo, chan_hi))])
                last.then_inc(ring_full, 1)

            def by_channel(dst, w_hi, w_lo, a_h, a_l):
                for j in range(2):
                    cols = slice(j * HALF, (j + 1) * HALF)
                    last = products(dst[:, cols], [
                        (l[cc], r[:, cc, cols]) for cc in range(CC)
                        for l, r in ((w_hi, a_h), (w_hi, a_l), (w_lo, a_h))])
                return last

            def by_token(dst, half, w_hi, w_lo):
                for t in range(JT // 2):
                    tok = slice((half * JT // 2 + t) * P, (half * JT // 2 + t + 1) * P)
                    last = products(dst[:, t * C:(t + 1) * C], [
                        (l[:, cc, tok], r[cc]) for cc in range(CC)
                        for l, r in ((chan_hi, w_hi), (chan_hi, w_lo), (chan_lo, w_hi))])
                return last

            def filler(name):
                dst = take_ring(name)
                if name in ("w0", "w1"):
                    if name == "w0":
                        pe.wait_ge(w_loaded, 15 * 16)
                        pe.wait_ge(const_made, 5)
                    cc = int(name[1])
                    for t in range(6):
                        last = nc.tensor.transpose(dst[:, t * P:(t + 1) * P], raw_wp[:, t, cc * P:(cc + 1) * P], ident[:, :])
                elif name in ("w2", "w3"):
                    raw = raw_wo if name == "w2" else raw_pj
                    for cc in range(CC):
                        for a in range(2):
                            last = nc.tensor.transpose(dst[:, cc * C + a * P:cc * C + (a + 1) * P],
                                                       raw[:, a, cc * P:(cc + 1) * P], ident[:, :])
                elif name == "w4":
                    for m in range(CC):
                        last = products(dst[:, m * C:(m + 1) * C], [
                            (raw_l1[:, a, m * P:(m + 1) * P], raw_l1[:, 2 + a, :]) for a in range(2)])
                elif name == "w5":
                    pe.wait_ge(lo_done, at.of("lo_done", "w3"))
                    for m in range(CC):
                        last = products(dst[:, m * C:(m + 1) * C], [
                            (raw_l1[:, 4 + a, m * P:(m + 1) * P], pj_t[:, a, :]) for a in range(2)])
                elif name[0] in "QK":
                    t, pair = "QK".index(name[0]), int(name[1])
                    pe.wait_ge(split_hi, at.of("split_hi", "x1"))
                    pe.wait_ge(split_lo, at.of("split_lo", "x1"))
                    cols = slice(pair * P, (pair + 1) * P)
                    last = by_channel(dst, [wp_hi[:, cc, t, cols] for cc in range(CC)],
                                      [wp_lo[:, cc, t, cols] for cc in range(CC)], chan_hi, chan_lo)
                elif name[0] == "V":
                    last = by_token(dst, "ab".index(name[1]), [wp_hi[:, cc, 2, :] for cc in range(CC)],
                                    [wp_lo[:, cc, 2, :] for cc in range(CC)])
                elif name[0] == "W":
                    pe.wait_ge(split_hi, at.of("split_hi", "O1"))
                    pe.wait_ge(split_lo, at.of("split_lo", "O1"))
                    cols = slice(int(name[1]) * P, (int(name[1]) + 1) * P)
                    last = by_channel(dst, [wo_hi[:, cc, cols] for cc in range(CC)],
                                      [wo_lo[:, cc, cols] for cc in range(CC)], og_hi, og_lo)
                elif name == "G1":
                    pe.wait_ge(stats_done, at.of("stats_done", "s1"))
                    last = products(dst[:, 0:CC], [(gmean[:, :], mv[:, :, 0])])
                elif name == "G2":
                    pe.wait_ge(dev_done, at.of("dev_done", "dev"))
                    last = products(dst[:, 0:CC], [(gmean[:, :], spread[:, :])])
                elif name[0] == "g":
                    pe.wait_ge(split_hi, at.of("split_hi", "h1"))
                    pe.wait_ge(split_lo, at.of("split_lo", "h1"))
                    cols = slice(int(name[1]) * P, (int(name[1]) + 1) * P)
                    last = by_channel(dst, [a_hi[:, cc, cols] for cc in range(CC)],
                                      [a_lo[:, cc, cols] for cc in range(CC)], chan_hi, chan_lo)
                else:
                    last = by_token(dst, "ab".index(name[1]), [b_hi[:, cc, :] for cc in range(CC)],
                                    [b_lo[:, cc, :] for cc in range(CC)])
                last.then_inc(ring_full, 1)

            def transposes(s):
                u, it, _ = slots[s]["tile"]
                if it == 0:
                    pe.wait_ge(norm_act, at.of_tile("norm_act", (u, IT - 1, 0)))
                    pe.wait_ge(norm_pool, at.of_tile("norm_pool", (u, max(POOL_NORM), 0)))
                for u, jt in jts(slots, s):
                    i = ORDER["t_full"][kind].index((u, jt))
                    if i >= 2 or kind != PRO:
                        pe.wait_ge(tlo_done, at.base("t_full") + i - 1)
                    for q in range(IT):
                        last = nc.tensor.transpose(tbank[jt % 2][:, q * P:(q + 1) * P],
                                                   probs[:, buf(u, q), jt * P:(jt + 1) * P], ident[:, :])
                    last.then_inc(t_full, 1)

            def values(s):
                order = ORDER["acc_done"][kind]
                for u, jt in jts(slots, s):
                    i = ORDER["t_full"][kind].index((u, jt))
                    first, final = jt == 0, jt == JT - 1
                    if first:
                        k = order.index(u)
                        if u[0] == "L":
                            pe.wait_ge(acc_done, at.base("acc_done") + k)
                        elif kind != PRO and k < 2:
                            pe.wait_ge(acc_done, at.base("acc_done"))
                        elif k >= 2:
                            pe.wait_ge(acc_done, at.base("acc_done") + k - 1)
                        if u == ("H", 0, 0):
                            pe.wait_ge(lo_done, at.of("lo_done", "Vb"))
                        if u == ("H", 3, 0):
                            pe.wait_ge(v3_lo, at.base("v3_lo"))
                        if u == ("L", 0, 0):
                            pe.wait_ge(lo_done, at.of("lo_done", "vb"))
                    pe.wait_ge(thi_done, at.base("t_full") + i + 1)
                    hi, lo = pt_hi[:, jt % 4, :], pt_lo[:, jt % 4, :]
                    if u[0] == "H":
                        v = v_st[:, u[1], jt, :]
                        nc.tensor.matmul(acc[u[2]][:, :], v, hi, start=first, stop=False)
                        pe.wait_ge(tlo_done, at.base("t_full") + i + 1)
                        last = nc.tensor.matmul(acc[u[2]][:, :], v, lo, start=False, stop=final)
                    else:
                        for m in range(CC):
                            o = slice(m * P, (m + 1) * P)
                            products(acc[m][:, :], [(v1_hi[:, jt, o], hi), (v1_lo[:, jt, o], hi)],
                                     start=first, stop=False)
                        pe.wait_ge(tlo_done, at.base("t_full") + i + 1)
                        for m in range(CC):
                            o = slice(m * P, (m + 1) * P)
                            last = products(acc[m][:, :], [(v1_hi[:, jt, o], lo)], start=False, stop=final)
                    last.then_inc(pv_done, 1)

            for s, sl in enumerate(slots):
                todo = value_slots(slots, s)
                if todo[:1] == [s - LAG]:
                    values(s - LAG)
                if sl["tile"]:
                    transposes(s)
                rest = [v for v in todo if v != s - LAG]
                for v in rest[:-1]:
                    values(v)
                if sl["fill"]:
                    filler(sl["fill"])
                if sl["score"]:
                    scores(sl["score"])
                for v in rest[-1:]:
                    values(v)

        def act_part(act, kind, n):
            at = At(kind, n)
            slots = SLOTS[kind]

            def upper(dst, src, **kw):
                return nc.scalar.activation(dst, src, ACT.Identity, **kw)

            def exponent(tile):
                u, it, _ = tile
                act.wait_ge(max_done, at.of("max_done", tile))
                free_probs(act, at, tile)
                b = buf(u, it)
                nc.scalar.activation(probs[:, b, :], ring[ring_of(at, tile)][:, :], ACT.Exp, bias=negmax[:, b:b + 1],
                                     accum_out=den[:, b:b + 1]).then_inc(exp_done, 1)

            def normalise(tile):
                b = buf(*tile[:2])
                act.wait_ge(rden_done, at.of("rden_done", tile))
                nc.scalar.activation(probs[:, b, :], probs[:, b, :], ACT.Copy,
                                     scale=rden[:, b:b + 1]).then_inc(norm_act, 1)

            def fill_hi(name):
                src = ring[at.ring_buffer(name)]
                act.wait_ge(ring_full, at.of("ring_full", name))
                if name in ("w0", "w1"):
                    cc = int(name[1])
                    upper(wp_hi[:, cc, 0, :], src[:, 0:C], scale=Q_SCALE)
                    last = upper(wp_hi[:, cc, 1:3, :], src[:, C:3 * C].rearrange("p (t c) -> p t c", t=2))
                elif name == "w2":
                    last = upper(wo_hi[:, :, :], src[:, 0:2 * C].rearrange("p (t c) -> p t c", t=2))
                elif name == "w3":
                    last = upper(pj_t, src[:, 0:2 * C].rearrange("p (t c) -> p t c", t=2))
                elif name == "w4":
                    last = upper(a_hi[:, :, :], src[:, 0:2 * C].rearrange("p (t c) -> p t c", t=2), scale=L1_SCALE)
                elif name == "w5":
                    last = upper(b_hi[:, :, :], src[:, 0:2 * C].rearrange("p (t c) -> p t c", t=2))
                elif name[0] in "QK":
                    t, pair = "QK".index(name[0]), int(name[1])
                    dst = (q_st, k_hh)[t]
                    if kind == PRO:
                        if name == "Q0":
                            act.wait_ge(bias_scaled, 1)
                    else:
                        if pair == 0:
                            act.wait_ge(ring_full, at.base("ring_full") - ring_back(at, (("H", 1, 1), IT - 1, 0)))
                        else:
                            act.wait_ge(ring_full, at.of("ring_full", (("H", 3, 1), IT - 1, 0)))
                        if t == 1:
                            act.wait_ge(k_dup[pair], (projections(kind, n) - 1) * 4 * 16)
                    for hh in range(2):
                        rows = slice(D * hh, D * hh + D)
                        last = upper(dst[rows, 2 * pair + hh, :], src[rows, :], bias=bias0[rows, t, pair:pair + 1])
                elif name[0] == "V":
                    half = "ab".index(name[1])
                    if kind != PRO:
                        act.wait_ge(pv_done, at.of("pv_done", (("H", 2, 1), JT - 1)))
                    jt = slice(half * JT // 2, (half + 1) * JT // 2)
                    view = src[:, :].rearrange("p (j h d) -> p j h d", h=HEADS, d=D)
                    for h in range(HEADS - 1):
                        upper(v_st[:, h, jt, 0:D], view[:, :, h, :])
                    stage = x_stage[:, 0:JT * D].rearrange("p (j d) -> p j d", d=D)
                    if name == "Va":
                        act.wait_ge(split_lo, at.of("split_lo", "x1"))
                    last = nc.scalar.activation(stage[:, jt, :], view[:, :, HEADS - 1, :], ACT.Identity)
                elif name[0] == "g":
                    last = upper(og_hi[:, int(name[1]), :], src[:, :])
                else:
                    half = "ab".index(name[1])
                    last = upper(v1_hi[:, half * JT // 2:(half + 1) * JT // 2, :],
                                 src[:, :].rearrange("p (j c) -> p j c", c=C))
                last.then_inc(hi_done, 1)

            def task(name):
                if name in ("x0", "x1"):
                    cc = int(name[1])
                    if kind == BODY and cc == 0:
                        act.wait_ge(ring_full, at.base("ring_full") - ring_back(at, (("L", 0, 1), IT - 1, 0)))
                    act.wait_ge(x_loaded, x_loads(kind, n, cc))
                    upper(chan_hi[:, cc, :], x_stage[:, :]).then_inc(split_hi, 1)
                elif name == "VS":
                    if kind == BODY:
                        act.wait_ge(pv_done, at.of("pv_done", (("H", 3, 1), JT - 1)))
                    act.wait_ge(hi_done, at.of("hi_done", "Vb"))
                    upper(v_st[:, HEADS - 1, :, 0:D],
                          x_stage[:, 0:JT * D].rearrange("p (j d) -> p j d", d=D)).then_inc(split_hi, 1)
                elif name in ("O0", "O1"):
                    pair = int(name[1])
                    if pair == 0:
                        act.wait_ge(acc_done, at.base("acc_done") - acc_back(at, ("H", 1, 1)))
                    else:
                        act.wait_ge(acc_done, at.of("acc_done", ("H", 3, 1)))
                    if pair == 0 and kind != PRO:
                        act.wait_ge(ring_full, at.base("ring_full"))
                    upper(og_hi[:, pair, :], o_f[:, pair, :]).then_inc(split_hi, 1)
                elif name in ("h0", "h1"):
                    cc = int(name[1])
                    act.wait_ge(h_done, at.of("h_done", name))
                    if kind == BODY and cc == 0:
                        act.wait_ge(ring_full, at.of("ring_full", "K1"))
                    upper(chan_hi[:, cc, :], x_stage[:, :]).then_inc(split_hi, 1)

            def take_lower(u):
                layer, h, c = u
                if layer == "L":
                    return
                act.wait_ge(pv_done, at.of("pv_done", (u, JT - 1)))
                if h == 0 and kind == BODY:
                    act.wait_ge(split_lo, at.of("split_lo", "O0"))
                if h == 2 and c == 0:
                    act.wait_ge(split_lo, at.base("split_lo"))
                nc.scalar.activation(o_f[D * (h % 2):D * (h % 2) + D, h // 2, c * HALF:(c + 1) * HALF],
                                     acc[c][D:2 * D, :], ACT.Identity).then_inc(acc_lower, 1)

            if kind == PRO:
                act.wait_ge(vec_loaded, 10 * 16)
                nc.scalar.activation(bias0[:, 0, :], bias0[:, 0, :], ACT.Copy, scale=Q_SCALE).then_inc(bias_scaled, 1)
            for s, sl in enumerate(slots):
                done = finished(slots, s)
                last_slot = s == len(slots) - 1
                for u in [] if last_slot else done:
                    take_lower(u)
                if sl["tile"]:
                    for u, jt in jts(slots, s):
                        i = ORDER["t_full"][kind].index((u, jt))
                        act.wait_ge(t_full, at.base("t_full") + i + 1)
                        if i >= 4 or kind != PRO:
                            act.wait_ge(pv_done, at.base("t_full") + i + 1 - 4)
                        upper(pt_hi[:, jt % 4, :], tbank[jt % 2][:, :]).then_inc(thi_done, 1)
                for u in done if last_slot else []:
                    take_lower(u)
                tile = norm_tile(kind, s)
                if tile and tile[1] not in POOL_NORM:
                    normalise(tile)
                tile = softmax_tile(kind, s)
                if tile:
                    exponent(tile)
                if sl["fill"] and sl["fill"] not in NO_HI:
                    fill_hi(sl["fill"])
                for name in sl["do"]:
                    task(name)

        def dve_part(dve, kind, n):
            at = At(kind, n)
            slots = SLOTS[kind]
            links = [0]

            def link(instruction):
                links[0] += 1
                instruction.then_inc(chain, 1)
                dve.wait_ge(chain, image_passes(kind, n) * CHAIN + links[0])

            def lower(dst, src, hi, scale=None, bias=None):
                if scale is None and bias is None:
                    return nc.vector.tensor_tensor(dst, src, hi.bitcast(F32), ALU.subtract)
                if bias is None:
                    return nc.vector.scalar_tensor_tensor(dst, src, scale, hi.bitcast(F32), ALU.mult, ALU.subtract)
                return nc.vector.scalar_tensor_tensor(dst, src, bias, hi.bitcast(F32), ALU.add, ALU.subtract)

            def fill_lo(name):
                src = ring[at.ring_buffer(name)]
                if name in NO_HI:
                    dve.wait_ge(ring_full, at.of("ring_full", name))
                else:
                    dve.wait_ge(hi_done, at.of("hi_done", name))
                if name in ("w0", "w1"):
                    cc = int(name[1])
                    lower(wp_lo[:, cc, 0, :], src[:, 0:C], wp_hi[:, cc, 0, :], scale=Q_SCALE)
                    last = lower(wp_lo[:, cc, 1:3, :], src[:, C:3 * C].rearrange("p (t c) -> p t c", t=2),
                                 wp_hi[:, cc, 1:3, :])
                elif name == "w2":
                    last = lower(wo_lo[:, :, :], src[:, 0:2 * C].rearrange("p (t c) -> p t c", t=2), wo_hi[:, :, :])
                elif name == "w3":
                    last = nc.vector.memset(mhalf[:, :], -0.5)
                elif name == "w4":
                    last = lower(a_lo[:, :, :], src[:, 0:2 * C].rearrange("p (t c) -> p t c", t=2), a_hi[:, :, :],
                                 scale=L1_SCALE)
                elif name == "w5":
                    last = lower(b_lo[:, :, :], src[:, 0:2 * C].rearrange("p (t c) -> p t c", t=2), b_hi[:, :, :])
                elif name[0] == "Q":
                    pair = int(name[1])
                    for hh in range(2):
                        rows, other = slice(D * hh, D * hh + D), slice(D - D * hh, 2 * D - D * hh)
                        h = 2 * pair + hh
                        last = lower(q_st[other, h, :], src[rows, :], q_st[rows, h, :], bias=bias0[rows, 0, pair:pair + 1])
                elif name[0] == "K":
                    pair = int(name[1])
                    for hh in range(2):
                        rows, h = slice(D * hh, D * hh + D), 2 * pair + hh
                        last = lower(k_ll[rows, h, :], src[rows, :], k_hh[rows, h, :], bias=bias0[rows, 1, pair:pair + 1])
                elif name[0] == "V":
                    half = "ab".index(name[1])
                    jt = slice(half * JT // 2, (half + 1) * JT // 2)
                    view = src[:, :].rearrange("p (j h d) -> p j h d", h=HEADS, d=D)
                    for h in range(HEADS - 1):
                        last = lower(v_st[:, h, jt, D:2 * D], view[:, :, h, :], v_st[:, h, jt, 0:D])
                elif name[0] == "W":
                    m = int(name[1])
                    dve.wait_ge(resid_loaded, (image_passes(kind, n) + 1) * CC * 16)
                    last = nc.vector.scalar_tensor_tensor(resid[:, m, :], src[:, :], vecs[:, 0, m:m + 1],
                                                          resid[:, m, :], ALU.add, ALU.add)
                elif name == "G1":
                    last = nc.vector.tensor_copy(gm[:, :], src[:, 0:CC])
                elif name == "G2":
                    last = nc.vector.tensor_scalar(varp[:, :], src[:, 0:CC], EPS, None, ALU.add)
                elif name[0] == "g":
                    last = lower(og_lo[:, int(name[1]), :], src[:, :], og_hi[:, int(name[1]), :])
                else:
                    half = "ab".index(name[1])
                    jt = slice(half * JT // 2, (half + 1) * JT // 2)
                    last = lower(v1_lo[:, jt, :], src[:, :].rearrange("p (j c) -> p j c", c=C), v1_hi[:, jt, :])
                last.then_inc(lo_done, 1)
                if name == "G1":
                    dve.wait_ge(lo_done, at.of("lo_done", "G1"))
                    link(nc.vector.tensor_tensor(dev[:, :], mv[:, :, 0], gm[:, :], ALU.subtract))
                    link(nc.vector.tensor_tensor(dev2[:, :], dev[:, :], dev[:, :], ALU.mult))
                    nc.vector.tensor_tensor(spread[:, :], dev2[:, :], mv[:, :, 1], ALU.add).then_inc(dev_done, 1)

            def task(name):
                if name == "VS":
                    dve.wait_ge(split_hi, at.of("split_hi", "VS"))
                    stage = x_stage[:, 0:JT * D].rearrange("p (j d) -> p j d", d=D)
                    lower(v_st[:, HEADS - 1, :, D:2 * D], stage, v_st[:, HEADS - 1, :, 0:D]).then_inc(v3_lo, 1)
                elif name in ("s0", "s1"):
                    m = int(name[1])
                    dve.wait_ge(lo_done, at.of("lo_done", f"W{m}"))
                    nc.vector.bn_stats(bst[:, m, 0, :], resid[:, m, 0:HALF])
                    nc.vector.bn_stats(bst[:, m, 1, :], resid[:, m, HALF:HW])
                    dve.drain()
                    nc.vector.bn_aggr(mv[:, m, :], bst[:, m, :, :].rearrange("p a b -> p (a b)")).then_inc(stats_done, 1)
                elif name in ("h0", "h1"):
                    cc = int(name[1])
                    if cc == 0:
                        dve.wait_ge(rstd_done, at.of("rstd_done", "rstd"))
                        link(nc.vector.tensor_tensor(ga[:, :], rstd[:, :], vecs[:, 1, :], ALU.mult))
                        link(nc.vector.tensor_tensor(gam[:, :], gm[:, :], ga[:, :], ALU.mult))
                        link(nc.vector.tensor_tensor(gb[:, :], vecs[:, 2, :], gam[:, :], ALU.subtract))
                    else:
                        dve.wait_ge(split_lo, at.of("split_lo", "h0"))
                    nc.vector.tensor_scalar(x_stage[:, :], resid[:, cc, :], ga[:, cc:cc + 1], gb[:, cc:cc + 1],
                                            ALU.mult, ALU.add).then_inc(h_done, 1)

            def take_result(u):
                layer, h, c = u
                cols = slice(c * HALF, (c + 1) * HALF)
                if layer == "H":
                    dve.wait_ge(acc_lower, at.of("acc_lower", u))
                    rows = slice(D * (h % 2), D * (h % 2) + D)
                    o = o_f[rows, h // 2, cols]
                    nc.vector.scalar_tensor_tensor(o, acc[c][0:D, :], bias0[rows, 2, h // 2:h // 2 + 1], o,
                                                   ALU.add, ALU.add).then_inc(acc_done, 1)
                else:
                    dve.wait_ge(pv_done, at.of("pv_done", (u, JT - 1)))
                    for m in range(CC):
                        last = nc.vector.scalar_tensor_tensor(resid[:, m, cols], acc[m][:, :], vecs[:, 3, m:m + 1],
                                                              resid[:, m, cols], ALU.add, ALU.add)
                    last.then_inc(acc_done, 1)

            if kind == PRO:
                dve.wait_ge(vec_loaded, 10 * 16)
            for s, sl in enumerate(slots):
                tile = softmax_tile(kind, s)
                if tile:
                    b = buf(*tile[:2])
                    dve.wait_ge(ring_full, ring_value(at, tile))
                    nc.vector.tensor_reduce(negmax[:, b:b + 1], ring[ring_of(at, tile)][:, :], axis=AX.X, op=ALU.max,
                                            negate=True).then_inc(max_done, 1)
                tile = norm_tile(kind, s)
                if tile:
                    b = buf(*tile[:2])
                    dve.wait_ge(exp_done, at.of_tile("exp_done", tile))
                    nc.vector.reciprocal(rden[:, b:b + 1], den[:, b:b + 1]).then_inc(rden_done, 1)
                done = finished(slots, s)
                urgent = s + 1 < len(slots) and any(
                    slots[v]["tile"][0][0] == "L" for v in value_slots(slots, s + 1))
                for u in done if urgent else []:
                    take_result(u)
                if sl["tile"]:
                    for u, jt in jts(slots, s):
                        i = ORDER["t_full"][kind].index((u, jt))
                        dve.wait_ge(thi_done, at.base("t_full") + i + 1)
                        lower(pt_lo[:, jt % 4, :], tbank[jt % 2][:, :], pt_hi[:, jt % 4, :]).then_inc(tlo_done, 1)
                for u in [] if urgent else done:
                    take_result(u)
                if sl["fill"]:
                    fill_lo(sl["fill"])
                for name in sl["do"]:
                    task(name)

        def pool_part(pool, kind, n):
            at = At(kind, n)
            slots = SLOTS[kind]
            if kind == PRO:
                pool.memset(ident[:, :], 0.0).then_inc(const_made, 1)
                pool.memset(gmean[:, :], 1.0 / GSIZE).then_inc(const_made, 1)
                pool.wait_ge(const_made, 2)
                pool.affine_select(out=ident[:, :], in_=ident[:, :], compare_op=ALU.not_equal, fill=1.0, base=0,
                                   pattern=[[-1, P]], channel_multiplier=1).then_inc(const_made, 1)
                g = gmean[:, :].rearrange("p (g c) -> p g c", c=GSIZE)
                pool.affine_select(out=g, in_=g, compare_op=ALU.is_ge, fill=0.0, base=0,
                                   pattern=[[-GSIZE, P // GSIZE], [0, GSIZE]], channel_multiplier=1).then_inc(const_made, 1)
                pool.wait_ge(const_made, 4)
                pool.affine_select(out=g, in_=g, compare_op=ALU.is_ge, fill=0.0, base=GSIZE - 1,
                                   pattern=[[GSIZE, P // GSIZE], [0, GSIZE]], channel_multiplier=-1).then_inc(const_made, 1)
            for s, sl in enumerate(slots):
                tile = norm_tile(kind, s)
                if tile and tile[1] in POOL_NORM:
                    b = buf(*tile[:2])
                    pool.wait_ge(rden_done, at.of("rden_done", tile))
                    pool.tensor_tensor(probs[:, b, :], probs[:, b, :], rden[:, b:b + 1].to_broadcast([P, HW]), ALU.mult).then_inc(norm_pool, 1)
                if sl["fill"] == "G2":
                    pool.wait_ge(lo_done, at.of("lo_done", "G2"))
                    pool.tensor_tensor(rstd[:, :], varp[:, :], mhalf[:, :], ALU.pow).then_inc(rstd_done, 1)
                for name in sl["do"]:
                    if name[0] in "xOh":
                        cc = int(name[1])
                        hi, lo, src = ((og_hi, og_lo, o_f[:, cc, :]) if name[0] == "O" else
                                       (chan_hi, chan_lo, x_stage[:, :]))
                        pool.wait_ge(split_hi, at.of("split_hi", name))
                        pool.tensor_tensor(lo[:, cc, :], src, hi[:, cc, :].bitcast(F32), ALU.subtract).then_inc(split_lo, 1)

        def ring_back(at, key):
            before = [BODY] if at.kind == LAST else [PRO, BODY]
            found = {len(ORDER["ring_full"][k]) - ORDER["ring_full"][k].index(key) - 1
                     for k in before if key in ORDER["ring_full"][k]}
            return min(found)

        def acc_back(at, unit):
            before = [BODY] if at.kind == LAST else [PRO, BODY]
            return min(len(ORDER["acc_done"][k]) - ORDER["acc_done"][k].index(unit) - 1 for k in before)

        def ring_value(at, tile):
            if tile in ORDER["ring_full"][at.kind]:
                return at.of("ring_full", tile)
            return at.of("ring_full", (tile[0], tile[1], 1), previous=True)

        def ring_of(at, tile):
            if tile in ORDER["ring_full"][at.kind]:
                return at.ring_buffer(tile)
            first = 0 if at.kind == PRO else len(ORDER["ring_full"][PRO])
            return (first - 1 - at.back("ring_full", (tile[0], tile[1], 1))) % 2

        def free_probs(act, at, tile):
            done = ORDER["t_full"][at.kind]
            u, it, gen = tile
            if gen == 1:
                units = [t[0] for t in (sl["tile"] for sl in SLOTS[at.kind]) if t and t[1] == 0]
                old = units[-2] if u[2] == 0 else units[-1]
                act.wait_ge(t_full, at.of("t_full", (old, JT - 1)))
                return
            units = [t[0] for t in (sl["tile"] for sl in SLOTS[at.kind]) if t and t[1] == 0]
            k = units.index(u) - 2
            if k >= 0:
                act.wait_ge(t_full, at.of("t_full", (units[k], JT - 1)))
            elif at.kind != PRO:
                act.wait_ge(t_full, at.base("t_full") + (k + 1) * JT)

        def whole(engine, part):
            part(engine, PRO, 0)
            with engine.Fori(0, LOOPS) as n:
                part(engine, BODY, n)
            part(engine, LAST, B - 1)

        @block.sync
        def _(sp):
            whole(sp, sp_part)

        @block.gpsimd
        def _(pool):
            whole(pool, pool_part)

        @block.scalar
        def _(act):
            whole(act, act_part)

        @block.vector
        def _(dve):
            whole(dve, dve_part)

        @block.tensor
        def _(pe):
            whole(pe, pe_part)


_INS = ['x', 'L0_conv_Wp', 'L0_conv_bp', 'L0_conv_Wo', 'L0_conv_bo', 'L1_conv_norm_w', 'L1_conv_norm_b',
        'L1_conv_qkv_w', 'L1_conv_proj_w', 'L1_conv_proj_b']
_OUTS = [((B, C, 32, 32), 'float32')]


def kernel(**inputs):
    import numpy as _np
    import concourse.bacc as _bacc
    from concourse import mybir as _mybir
    from concourse.bass_utils import run_bass_kernel_spmd as _run

    nc = _bacc.Bacc("TRN2", target_bir_lowering=False, num_devices=1)
    arrays, args = {}, []
    for name in _INS:
        a = _np.ascontiguousarray(inputs[name])
        arrays[f"in_{name}_dram"] = a
        args.append(nc.dram_tensor(f"in_{name}_dram", a.shape, _mybir.dt.from_np(a.dtype), kind="ExternalInput").ap())
    for i, (shape, dtype) in enumerate(_OUTS):
        dt = _mybir.dt.from_np(_np.dtype(dtype))
        args.append(nc.dram_tensor(f"out_{i}_dram", shape, dt, kind="ExternalOutput").ap())
    build_program(nc, *args)
    r = _run(nc, [arrays], core_ids=[0])
    got = tuple(r.results[0][f"out_{i}_dram"] for i in range(len(_OUTS)))
    return got[0]
```

```python
import numpy as np
import concourse.bass as bass
import concourse.mybir as mybir
from contextlib import ExitStack

F32 = mybir.dt.float32
F32R = mybir.dt.float32r
ALU = mybir.AluOpType
ACT = mybir.ActivationFunctionType
AX = mybir.AxisListType

P = 128
B, C, HW = 16, 256, 32 * 32
HEADS, D = 4, 64
CC = C // P
JT = HW // P
HALF = 512
IT = HALF // P
GROUPS = 8
GSIZE = C // GROUPS
EPS = 1e-5
Q_SCALE = D ** -0.5
L1_SCALE = C ** -0.5
LEAD = 6
LAG = 2
POOL_NORM = (0, 1, 2)

PRO, BODY, LAST = "prologue", "body", "last"
LOOPS = B - 1



def heads(*hs):
    return [("H", h, c) for h in hs for c in range(2)]


L1_UNITS = [("L", 0, 1), ("L", 0, 0)]
REST_UNITS = [("H", 2, 1)] + heads(3)
NEXT_TILES = [(REST_UNITS[i // IT], i % IT) for i in range(LEAD)]


def tiles_of(units, gen):
    return [(u, it, gen) for u in units for it in range(IT)]


def make_slots(kind):
    first_units = heads(0, 1) + [("H", 2, 0)]
    if kind == PRO:
        lead_in, units, gap = 12 + LEAD, first_units, None
        fill = {0: "w0", 1: "w1", 2: "w2", 3: "w3", 4: "w4", 5: "w5",
                6: "K0", 7: "Q0", 8: "Va", 9: "Vb", 10: "Q1", 11: "K1"}
        stat = {}
        do = {2: ["x0"], 4: ["x1"], 13: ["VS"], 20: ["y0"], 24: ["y1"]}
    elif kind == BODY:
        lead_in, units, gap = 0, REST_UNITS + first_units + L1_UNITS, None
        fill = {0: "K0", 2: "Q0", 7: "Q1", 8: "Va", 10: "Vb", 12: "K1", 15: "W0", 17: "W1",
                23: "g0", 24: "g1", 28: "va", 30: "vb"}
        stat = {19: "G1", 20: "G2"}
        do = {0: ["O0"], 10: ["O1a"], 13: ["O1b"], 14: ["VS"], 16: ["s0"], 18: ["s1"],
              21: ["h0"], 22: ["h1"], 34: ["y0"], 37: ["y1"]}
    else:
        lead_in, units, gap = 0, REST_UNITS + L1_UNITS, (12, 14)
        fill = {14: "W0", 15: "W1", 18: "g0", 19: "g1", 20: "va", 22: "vb"}
        stat = {16: "G1", 17: "G2"}
        do = {0: ["O0"], 10: ["O1a"], 13: ["O1b"], 14: ["s0"], 15: ["s1"], 17: ["h0", "h1"]}
    real = tiles_of(units, 0)
    order = [None] * lead_in + real
    if gap:
        order = order[:gap[0]] + [None] * gap[1] + order[gap[0]:]
    following = [] if kind == LAST else [(u, it, 1) for u, it in NEXT_TILES]
    slots = []
    for s, t in enumerate(order):
        a = s + LEAD
        ahead = order[a] if a < len(order) else (following[a - len(order)] if a - len(order) < len(following) else None)
        slots.append(dict(tile=t, score=ahead, fill=fill.get(s), stat=stat.get(s),
                          do=do.get(s, [])))
    return slots


SLOTS = {k: make_slots(k) for k in (PRO, BODY, LAST)}


def value_slots(slots, s):
    out = [s - LAG] if s >= LAG and slots[s - LAG]["tile"] else []
    if s == len(slots) - 1:
        out += [k for k in range(s - LAG + 1, s + 1) if slots[k]["tile"]]
    return out


def finished(slots, s):
    return [slots[k]["tile"][0] for k in value_slots(slots, s) if slots[k]["tile"][1] == IT - 1]




def ring_order(kind):
    out = []
    for sl in SLOTS[kind]:
        out += [sl["fill"]] if sl["fill"] else []
        out += [sl["score"]] if sl["score"] else []
    return out


def softmax_tile(kind, s):
    if s == 0:
        return None if kind == PRO else (*NEXT_TILES[-1], 0)
    return SLOTS[kind][s - 1]["score"]


def norm_tile(kind, s):
    if s == 0:
        return None if kind == PRO else (*NEXT_TILES[-2], 0)
    return softmax_tile(kind, s - 1)


def softmax_order(kind):
    return [t for t in (softmax_tile(kind, s) for s in range(len(SLOTS[kind]))) if t]


def norm_order(kind):
    return [t for t in (norm_tile(kind, s) for s in range(len(SLOTS[kind]))) if t]


def per_slot(kind, of):
    return [x for s in range(len(SLOTS[kind])) for x in of(SLOTS[kind], s)]


def jts(slots, k):
    u, it, _ = slots[k]["tile"]
    return [(u, 2 * it), (u, 2 * it + 1)]


def order_of(pick):
    return {k: pick(k) for k in (PRO, BODY, LAST)}


def done_fills(kind, skip=()):
    return [sl["fill"] for sl in SLOTS[kind] if sl["fill"] and sl["fill"] not in skip]


def tasks(kind, names):
    return [d for sl in SLOTS[kind] for d in sl["do"] if d in names]


NEXT_X = ("y0", "y1")
NO_HI = ("W0", "W1")

ORDER = {
    "ring_full": order_of(ring_order),
    "t_full": order_of(lambda k: per_slot(k, lambda sl, s: jts(sl, s) if sl[s]["tile"] else [])),
    "pv_done": order_of(lambda k: per_slot(k, lambda sl, s: [j for v in value_slots(sl, s) for j in jts(sl, v)])),
    "max_done": order_of(softmax_order),
    "exp_done": order_of(softmax_order),
    "rden_done": order_of(norm_order),
    "norm_act": order_of(lambda k: [t for t in norm_order(k) if t[1] not in POOL_NORM]),
    "norm_pool": order_of(lambda k: [t for t in norm_order(k) if t[1] in POOL_NORM]),
    "hi_done": order_of(lambda k: done_fills(k, NO_HI)),
    "lo_done": order_of(done_fills),
    "acc_lower": order_of(lambda k: [u for u in per_slot(k, finished) if u[0] == "H"]),
    "acc_done": order_of(lambda k: per_slot(k, finished)),
    "split_hi": order_of(lambda k: tasks(k, ("x0", "x1", "y0", "y1", "VS", "O0", "O1a", "O1b", "h0", "h1"))),
    "split_lo": order_of(lambda k: tasks(k, ("x0", "x1", "y0", "y1", "O0", "O1a", "O1b", "h0", "h1"))),
    "v3_lo": order_of(lambda k: tasks(k, ("VS",))),
    "h_done": order_of(lambda k: tasks(k, ("h0", "h1"))),
    "stats_done": order_of(lambda k: tasks(k, ("s0", "s1"))),
    "dev_done": order_of(lambda k: ["dev"] if k != PRO else []),
    "stat_full": order_of(lambda k: [sl["stat"] for sl in SLOTS[k] if sl["stat"]]),
    "stat_taken": order_of(lambda k: [sl["stat"] for sl in SLOTS[k] if sl["stat"]]),
    "rstd_done": order_of(lambda k: ["rstd"] if k != PRO else []),
}
assert len(ORDER["ring_full"][BODY]) % 2 == 0


class At:

    def __init__(self, kind, n):
        self.kind, self.n = kind, n

    def base(self, name):
        o = ORDER[name]
        if self.kind == PRO:
            return 0
        if self.kind == BODY:
            return self.n * len(o[BODY]) + len(o[PRO])
        return LOOPS * len(o[BODY]) + len(o[PRO]) - len([k for k in o[BODY] if k in NEXT_X])

    def back(self, name, key):
        before = [BODY] if self.kind == LAST else [PRO, BODY]
        found = {len(ORDER[name][k]) - ORDER[name][k].index(key) - 1 for k in before}
        assert len(found) == 1, (name, key, found)
        return found.pop()

    def of(self, name, key, previous=False):
        if previous:
            return self.base(name) - self.back(name, key)
        return self.base(name) + ORDER[name][self.kind].index(key) + 1

    def of_tile(self, name, tile):
        if tile in ORDER[name][self.kind]:
            return self.of(name, tile)
        return self.of(name, (tile[0], tile[1], 1), previous=True)

    def ring_buffer(self, key):
        first = 0 if self.kind == PRO else len(ORDER["ring_full"][PRO])
        return (first + ORDER["ring_full"][self.kind].index(key)) % 2


def build_program(nc, x, Wp, bp, Wo, bo, norm_w, norm_b, qkv_w, proj_w, proj_b, out):
    x_t = x.rearrange("b (cc p) h w -> b cc p (h w)", p=P)
    out_t = out.rearrange("b (cc p) h w -> b cc p (h w)", p=P)

    ctx = ExitStack()
    with ctx:
        def sb(name, shape, dt=F32):
            return ctx.enter_context(nc.sbuf_tensor(name, shape, dt))

        def sem(name):
            return ctx.enter_context(nc.semaphore(name))

        x_stage = sb("x_stage", [P, HW])
        resid = sb("resid", [P, CC, HW])
        chan_hi = sb("chan_hi", [P, CC, HW], F32R)
        chan_lo = sb("chan_lo", [P, CC, HW], F32R)
        q_st = sb("q_st", [P, HEADS, HW], F32R)
        k_hh = sb("k_hh", [P, HEADS, HW], F32R)
        k_ll = sb("k_ll", [P, HEADS, HW], F32R)
        v_st = sb("v_st", [P, HEADS, JT, 2 * D], F32R)
        probs = sb("probs", [P, 2 * IT, HW])
        pt_hi = sb("pt_hi", [P, 4, HALF], F32R)
        pt_lo = sb("pt_lo", [P, 4, HALF], F32R)
        o_f = sb("o_f", [P, CC, HW])
        og_hi = sb("og_hi", [P, CC, HW], F32R)
        og_lo = sb("og_lo", [P, CC, HW], F32R)
        v1_hi = sb("v1_hi", [P, JT, C], F32R)
        v1_lo = sb("v1_lo", [P, JT, C], F32R)
        wp_hi = sb("wp_hi", [P, CC, 3, C], F32R)
        wp_lo = sb("wp_lo", [P, CC, 3, C], F32R)
        wo_hi = sb("wo_hi", [P, CC, C], F32R)
        wo_lo = sb("wo_lo", [P, CC, C], F32R)
        a_hi = sb("a_hi", [P, CC, C], F32R)
        a_lo = sb("a_lo", [P, CC, C], F32R)
        b_hi = sb("b_hi", [P, CC, C], F32R)
        b_lo = sb("b_lo", [P, CC, C], F32R)
        bias0 = sb("bias0", [P, 3, CC])
        vecs = sb("vecs", [P, 4, CC])
        ident = sb("ident", [P, P])
        gmean = sb("gmean", [P, P])
        negmax = sb("negmax", [P, 2 * IT])
        den = sb("den", [P, 2 * IT])
        rden = sb("rden", [P, 2 * IT])
        bst = sb("bst", [P, CC, 2, 6])
        mv = sb("mv", [P, CC, 2])
        gm = sb("gm", [P, CC])
        dev = sb("dev", [P, CC])
        dev2 = sb("dev2", [P, CC])
        spread = sb("spread", [P, CC])
        varp = sb("varp", [P, CC])
        mhalf = sb("mhalf", [P, CC])
        rstd = sb("rstd", [P, CC])
        ga = sb("ga", [P, CC])
        gam = sb("gam", [P, CC])
        gb = sb("gb", [P, CC])
        raw_wp = probs[:, 0:2, :].rearrange("p a (b c) -> p (a b) c", c=C)
        raw_wo = probs[:, 2, 0:2 * C].rearrange("p (a c) -> p a c", c=C)
        raw_pj = probs[:, 2, 2 * C:4 * C].rearrange("p (a c) -> p a c", c=C)
        raw_l1 = probs[:, 3:5, :].rearrange("p a (b c) -> p (a b) c", c=C)
        pj_t = probs[:, 5, 0:2 * C].rearrange("p (a c) -> p a c", c=C)

        ring = [ctx.enter_context(nc.psum_tensor(f"ring{i}", [P, HW], F32)) for i in range(2)]
        tbank = [ctx.enter_context(nc.psum_tensor(f"tbank{i}", [P, HALF], F32)) for i in range(2)]
        acc = [ctx.enter_context(nc.psum_tensor(f"acc{i}", [P, HALF], F32)) for i in range(2)]

        S = {name: sem(name) for name in ORDER}
        ring_full, t_full, pv_done = S["ring_full"], S["t_full"], S["pv_done"]
        max_done, exp_done, rden_done = S["max_done"], S["exp_done"], S["rden_done"]
        norm_act, norm_pool = S["norm_act"], S["norm_pool"]
        hi_done, lo_done, acc_lower, acc_done = S["hi_done"], S["lo_done"], S["acc_lower"], S["acc_done"]
        split_hi, split_lo, v3_lo, h_done = S["split_hi"], S["split_lo"], S["v3_lo"], S["h_done"]
        stat_full, stat_taken = S["stat_full"], S["stat_taken"]
        stats_done, dev_done, rstd_done = S["stats_done"], S["dev_done"], S["rstd_done"]
        thi_done, tlo_done = sem("thi_done"), sem("tlo_done")
        chain = sem("chain")
        x_loaded, resid_loaded = sem("x_loaded"), sem("resid_loaded")
        k_dup = [sem("k_dup0"), sem("k_dup1")]
        q_moved = [sem("q_moved0"), sem("q_moved1")]
        stored = sem("stored")
        w_loaded, vec_loaded, const_made, bias_scaled = sem("w_loaded"), sem("vec_loaded"), sem("const_made"), sem("bias_scaled")
        K_COPIES, Q_COPIES = 6, 3
        CHAIN = 5

        block = ctx.enter_context(nc.Block())

        def buf(unit, it):
            return unit[2] * IT + it

        def final_pass(kind, n):
            return kind == BODY and isinstance(n, int)

        def stage_tasks(sl, kind, n):
            return [d for d in sl["do"] if not (final_pass(kind, n) and d in NEXT_X)]

        def attention_part(name):
            half = "ab".find(name[2:]) if name[2:] else None
            return int(name[1]), slice(0, HW) if half is None else slice(half * HALF, (half + 1) * HALF)

        def image_passes(kind, n):
            return 0 if kind == PRO else n if kind == BODY else LOOPS

        def x_loads(kind, n, name):
            image = 0 if name[0] == "x" else 1 if kind == PRO else n + 2
            return 16 * (2 * image + int(name[1]) + 1)

        def projections(kind, n):
            return 1 if kind == PRO else n + 2

        def sp_part(sp, kind, n):
            at = At(kind, n)

            def load_x(image, cc):
                sp.dma_start(x_stage[:, :], x_t[image, cc]).then_inc(x_loaded, 16)

            low, high = slice(0, D), slice(D, 2 * D)

            def copy(dst, src, done):
                sp.dma_start(dst, src).then_inc(done, 16)

            def duplicate_k(pair):
                sp.wait_ge(lo_done, at.of("lo_done", f"K{pair}"))
                even, odd, done = 2 * pair, 2 * pair + 1, projections(kind, n) * K_COPIES * 16
                for k in (k_hh, k_ll):
                    for half in (low, high):
                        copy(k[half, odd, :].bitcast(F32), k[high, even, :].bitcast(F32), k_dup[pair])
                sp.wait_ge(k_dup[pair], done - 2 * 16)
                for k in (k_hh, k_ll):
                    copy(k[high, even, :].bitcast(F32), k[low, even, :].bitcast(F32), k_dup[pair])

            def stack_q(pair):
                sp.wait_ge(lo_done, at.of("lo_done", f"Q{pair}"))
                even, odd, done = 2 * pair, 2 * pair + 1, projections(kind, n) * Q_COPIES * 16
                copy(q_st[low, odd, :].bitcast(F32), q_st[high, even, :].bitcast(F32), q_moved[pair])
                copy(q_st[high, odd, :].bitcast(F32), o_f[high, 0, :], q_moved[pair])
                sp.wait_ge(q_moved[pair], done - 16)
                copy(q_st[high, even, :].bitcast(F32), o_f[low, 0, :], q_moved[pair])

            def load_residual(image):
                sp.wait_ge(stored, (image * 4 + 1) * 16)
                for cc in range(CC):
                    sp.dma_start(resid[:, cc, :], x_t[image, cc]).then_inc(resid_loaded, 16)

            if kind == PRO:
                sp.sem_inc(stored, 16)
                load_x(0, 0)
                wp_v = Wp.rearrange("(h t d) c -> t h d c", h=HEADS, t=3)
                for t in range(3):
                    for h in range(HEADS):
                        sp.dma_start(raw_wp[D * (h % 2):D * (h % 2) + D, 2 * t + h // 2, :],
                                     wp_v[t, h]).then_inc(w_loaded, 16)
                sp.dma_start(raw_wo, Wo.rearrange("(a p) c -> p a c", p=P)).then_inc(w_loaded, 16)
                sp.dma_start(raw_pj, proj_w.rearrange("(a p) c -> p a c", p=P)).then_inc(w_loaded, 16)
                sp.dma_start(raw_l1[:, 0:6, :], qkv_w.rearrange("(a p) c -> p a c", p=P)).then_inc(w_loaded, 16)
                bp_v = bp.rearrange("(pr hh t d) -> hh d t pr", pr=2, hh=2, t=3)
                for hh in range(2):
                    for t in range(3):
                        sp.dma_start(bias0[D * hh:D * hh + D, t, :], bp_v[hh, :, t],
                                     allow_slow_non_contiguous=True).then_inc(vec_loaded, 16)
                for i, v in enumerate((bo, norm_w, norm_b, proj_b)):
                    sp.dma_start(vecs[:, i, :], v.rearrange("(a p) -> p a", p=P),
                                 allow_slow_non_contiguous=True).then_inc(vec_loaded, 16)
                sp.wait_ge(split_lo, at.of("split_lo", "x0"))
                load_x(0, 1)
            if kind == LAST:
                load_residual(B - 1)
            else:
                duplicate_k(0)
                stack_q(0)
                if kind == BODY:
                    load_residual(n)
                stack_q(1)
                duplicate_k(1)
            if kind != LAST and not final_pass(kind, n):
                image = 1 if kind == PRO else n + 2
                if kind == PRO:
                    sp.wait_ge(v3_lo, 1)
                else:
                    sp.wait_ge(split_lo, at.of("split_lo", "h1"))
                load_x(image, 0)
                sp.wait_ge(split_lo, at.of("split_lo", "y0"))
                load_x(image, 1)
            if kind != PRO:
                image = n if kind == BODY else B - 1
                for u in L1_UNITS:
                    sp.wait_ge(acc_done, at.of("acc_done", u))
                    cols = slice(u[2] * HALF, u[2] * HALF + HALF)
                    for cc in range(CC):
                        sp.dma_start(out_t[image, cc, :, cols], resid[:, cc, cols]).then_inc(stored, 16)
            if kind == LAST:
                sp.wait_ge(stored, (B * 4 + 1) * 16)

        def pe_part(pe, kind, n):
            at = At(kind, n)
            slots = SLOTS[kind]
            ring_keys = ORDER["ring_full"][kind]

            def products(dst, terms, start=True, stop=True):
                for i, (lhs, rhs) in enumerate(terms):
                    last = nc.tensor.matmul(dst, lhs, rhs, start=start and i == 0,
                                            stop=stop and i == len(terms) - 1)
                return last

            def take_ring(key):
                i = ring_keys.index(key)
                if i >= 2:
                    old, previous = ring_keys[i - 2], False
                elif kind == PRO:
                    return ring[at.ring_buffer(key)]
                else:
                    old, previous = ORDER["ring_full"][BODY][i - 2], True
                if isinstance(old, str):
                    pe.wait_ge(lo_done, at.of("lo_done", old))
                elif previous and old[:2] == NEXT_TILES[-1]:
                    pe.wait_ge(exp_done, at.of("exp_done", (*old[:2], 0)))
                else:
                    pe.wait_ge(exp_done, at.of("exp_done", old, previous))
                return ring[at.ring_buffer(key)]

            def scores(tile):
                (layer, h, c), it, gen = tile
                dst = take_ring(tile)
                q = slice((c * IT + it) * P, (c * IT + it + 1) * P)
                if layer == "H":
                    if c == 0 and it == 0 and h % 2 == 0:
                        pe.wait_ge(lo_done, at.of("lo_done", f"K{h // 2}"))
                        pe.wait_ge(k_dup[h // 2], projections(kind, n) * K_COPIES * 16)
                        pe.wait_ge(q_moved[h // 2], projections(kind, n) * Q_COPIES * 16)
                    for j in range(2):
                        keys = slice(j * HALF, (j + 1) * HALF)
                        last = products(dst[:, keys], [(q_st[:, h, q], k_hh[:, h, keys]),
                                                       (q_st[:, h, q], k_ll[:, h, keys])])
                else:
                    if tile[0] == L1_UNITS[0] and it == 0:
                        pe.wait_ge(lo_done, at.of("lo_done", "g1"))
                    for j in range(2):
                        keys = slice(j * HALF, (j + 1) * HALF)
                        last = products(dst[:, keys], [
                            (l[:, cc, q], r[:, cc, keys]) for cc in range(CC)
                            for l, r in ((og_hi, chan_hi), (og_hi, chan_lo), (og_lo, chan_hi))])
                last.then_inc(ring_full, 1)

            def by_channel(dst, w_hi, w_lo, a_h, a_l):
                for j in range(2):
                    cols = slice(j * HALF, (j + 1) * HALF)
                    last = products(dst[:, cols], [
                        (l[cc], r[:, cc, cols]) for cc in range(CC)
                        for l, r in ((w_hi, a_h), (w_hi, a_l), (w_lo, a_h))])
                return last

            def by_token(dst, half, w_hi, w_lo):
                for t in range(JT // 2):
                    tok = slice((half * JT // 2 + t) * P, (half * JT // 2 + t + 1) * P)
                    last = products(dst[:, t * C:(t + 1) * C], [
                        (l[:, cc, tok], r[cc]) for cc in range(CC)
                        for l, r in ((chan_hi, w_hi), (chan_hi, w_lo), (chan_lo, w_hi))])
                return last

            def filler(name):
                dst = take_ring(name)
                if name in ("w0", "w1"):
                    if name == "w0":
                        pe.wait_ge(w_loaded, 15 * 16)
                        pe.wait_ge(const_made, 5)
                    cc = int(name[1])
                    for t in range(6):
                        last = nc.tensor.transpose(dst[:, t * P:(t + 1) * P], raw_wp[:, t, cc * P:(cc + 1) * P], ident[:, :])
                elif name in ("w2", "w3"):
                    raw = raw_wo if name == "w2" else raw_pj
                    for cc in range(CC):
                        for a in range(2):
                            last = nc.tensor.transpose(dst[:, cc * C + a * P:cc * C + (a + 1) * P],
                                                       raw[:, a, cc * P:(cc + 1) * P], ident[:, :])
                elif name == "w4":
                    for m in range(CC):
                        last = products(dst[:, m * C:(m + 1) * C], [
                            (raw_l1[:, a, m * P:(m + 1) * P], raw_l1[:, 2 + a, :]) for a in range(2)])
                elif name == "w5":
                    pe.wait_ge(lo_done, at.of("lo_done", "w3"))
                    for m in range(CC):
                        last = products(dst[:, m * C:(m + 1) * C], [
                            (raw_l1[:, 4 + a, m * P:(m + 1) * P], pj_t[:, a, :]) for a in range(2)])
                elif name[0] in "QK":
                    t, pair = "QK".index(name[0]), int(name[1])
                    if kind == PRO:
                        pe.wait_ge(split_hi, at.of("split_hi", "x1"))
                        pe.wait_ge(split_lo, at.of("split_lo", "x1"))
                    elif name == "K0":
                        pe.wait_ge(split_hi, at.base("split_hi"))
                        pe.wait_ge(split_lo, at.base("split_lo"))
                    cols = slice(pair * P, (pair + 1) * P)
                    last = by_channel(dst, [wp_hi[:, cc, t, cols] for cc in range(CC)],
                                      [wp_lo[:, cc, t, cols] for cc in range(CC)], chan_hi, chan_lo)
                elif name[0] == "V":
                    last = by_token(dst, "ab".index(name[1]), [wp_hi[:, cc, 2, :] for cc in range(CC)],
                                    [wp_lo[:, cc, 2, :] for cc in range(CC)])
                elif name[0] == "W":
                    pe.wait_ge(split_hi, at.of("split_hi", "O1b"))
                    pe.wait_ge(split_lo, at.of("split_lo", "O1b"))
                    cols = slice(int(name[1]) * P, (int(name[1]) + 1) * P)
                    last = by_channel(dst, [wo_hi[:, cc, cols] for cc in range(CC)],
                                      [wo_lo[:, cc, cols] for cc in range(CC)], og_hi, og_lo)
                elif name[0] == "g":
                    pe.wait_ge(split_hi, at.of("split_hi", "h1"))
                    pe.wait_ge(split_lo, at.of("split_lo", "h1"))
                    cols = slice(int(name[1]) * P, (int(name[1]) + 1) * P)
                    last = by_channel(dst, [a_hi[:, cc, cols] for cc in range(CC)],
                                      [a_lo[:, cc, cols] for cc in range(CC)], chan_hi, chan_lo)
                else:
                    last = by_token(dst, "ab".index(name[1]), [b_hi[:, cc, :] for cc in range(CC)],
                                    [b_lo[:, cc, :] for cc in range(CC)])
                last.then_inc(ring_full, 1)

            def stat(name):
                if name == "G1":
                    pe.wait_ge(stats_done, at.of("stats_done", "s1"))
                    pe.wait_ge(acc_done, at.of("acc_done", ("H", 0, 0) if kind == BODY else ("H", 3, 1)))
                    moving = mv[:, :, 0]
                else:
                    pe.wait_ge(dev_done, at.of("dev_done", "dev"))
                    moving = spread[:, :]
                products(acc[0][:, 0:CC], [(gmean[:, :], moving)]).then_inc(stat_full, 1)

            def transposes(s):
                u, it, _ = slots[s]["tile"]
                if it == 0:
                    pe.wait_ge(norm_act, at.of_tile("norm_act", (u, IT - 1, 0)))
                    pe.wait_ge(norm_pool, at.of_tile("norm_pool", (u, max(POOL_NORM), 0)))
                for u, jt in jts(slots, s):
                    i = ORDER["t_full"][kind].index((u, jt))
                    if i >= 2 or kind != PRO:
                        pe.wait_ge(tlo_done, at.base("t_full") + i - 1)
                    for q in range(IT):
                        last = nc.tensor.transpose(tbank[jt % 2][:, q * P:(q + 1) * P],
                                                   probs[:, buf(u, q), jt * P:(jt + 1) * P], ident[:, :])
                    last.then_inc(t_full, 1)

            def values(s):
                order = ORDER["acc_done"][kind]
                for u, jt in jts(slots, s):
                    i = ORDER["t_full"][kind].index((u, jt))
                    first, final = jt == 0, jt == JT - 1
                    if first:
                        k = order.index(u)
                        if u[0] == "L":
                            pe.wait_ge(acc_done, at.base("acc_done") + k)
                        elif kind != PRO and k < 2:
                            pe.wait_ge(acc_done, at.base("acc_done"))
                        elif k >= 2:
                            pe.wait_ge(acc_done, at.base("acc_done") + k - 1)
                        if u == ("H", 0, 0):
                            pe.wait_ge(lo_done, at.of("lo_done", "Vb"))
                        if u == ("H", 1, 0) and kind == BODY or u == L1_UNITS[0] and kind == LAST:
                            pe.wait_ge(stat_taken, at.of("stat_taken", "G2"))
                        if u == ("H", 3, 0):
                            pe.wait_ge(v3_lo, at.base("v3_lo"))
                        if u == L1_UNITS[0]:
                            pe.wait_ge(lo_done, at.of("lo_done", "vb"))
                    pe.wait_ge(thi_done, at.base("t_full") + i + 1)
                    hi, lo = pt_hi[:, jt % 4, :], pt_lo[:, jt % 4, :]
                    if u[0] == "H":
                        v = v_st[:, u[1], jt, :]
                        nc.tensor.matmul(acc[u[2]][:, :], v, hi, start=first, stop=False)
                        pe.wait_ge(tlo_done, at.base("t_full") + i + 1)
                        last = nc.tensor.matmul(acc[u[2]][:, :], v, lo, start=False, stop=final)
                    else:
                        for m in range(CC):
                            o = slice(m * P, (m + 1) * P)
                            products(acc[m][:, :], [(v1_hi[:, jt, o], hi), (v1_lo[:, jt, o], hi)],
                                     start=first, stop=False)
                        pe.wait_ge(tlo_done, at.base("t_full") + i + 1)
                        for m in range(CC):
                            o = slice(m * P, (m + 1) * P)
                            last = products(acc[m][:, :], [(v1_hi[:, jt, o], lo)], start=False, stop=final)
                    last.then_inc(pv_done, 1)

            for s, sl in enumerate(slots):
                todo = value_slots(slots, s)
                if todo[:1] == [s - LAG]:
                    values(s - LAG)
                if sl["tile"]:
                    transposes(s)
                rest = [v for v in todo if v != s - LAG]
                for v in rest[:-1]:
                    values(v)
                if sl["stat"]:
                    stat(sl["stat"])
                if sl["fill"]:
                    filler(sl["fill"])
                if sl["score"]:
                    scores(sl["score"])
                for v in rest[-1:]:
                    values(v)

        def act_part(act, kind, n):
            at = At(kind, n)
            slots = SLOTS[kind]

            def upper(dst, src, **kw):
                return nc.scalar.activation(dst, src, ACT.Identity, **kw)

            def exponent(tile):
                u, it, _ = tile
                act.wait_ge(max_done, at.of("max_done", tile))
                free_probs(act, at, tile)
                b = buf(u, it)
                nc.scalar.activation(probs[:, b, :], ring[ring_of(at, tile)][:, :], ACT.Exp, bias=negmax[:, b:b + 1],
                                     accum_out=den[:, b:b + 1]).then_inc(exp_done, 1)

            def normalise(tile):
                b = buf(*tile[:2])
                act.wait_ge(rden_done, at.of("rden_done", tile))
                nc.scalar.activation(probs[:, b, :], probs[:, b, :], ACT.Copy,
                                     scale=rden[:, b:b + 1]).then_inc(norm_act, 1)

            def fill_hi(name):
                src = ring[at.ring_buffer(name)]
                act.wait_ge(ring_full, at.of("ring_full", name))
                if name in ("w0", "w1"):
                    cc = int(name[1])
                    upper(wp_hi[:, cc, 0, :], src[:, 0:C], scale=Q_SCALE)
                    last = upper(wp_hi[:, cc, 1:3, :], src[:, C:3 * C].rearrange("p (t c) -> p t c", t=2))
                elif name == "w2":
                    last = upper(wo_hi[:, :, :], src[:, 0:2 * C].rearrange("p (t c) -> p t c", t=2))
                elif name == "w3":
                    last = upper(pj_t, src[:, 0:2 * C].rearrange("p (t c) -> p t c", t=2))
                elif name == "w4":
                    last = upper(a_hi[:, :, :], src[:, 0:2 * C].rearrange("p (t c) -> p t c", t=2), scale=L1_SCALE)
                elif name == "w5":
                    last = upper(b_hi[:, :, :], src[:, 0:2 * C].rearrange("p (t c) -> p t c", t=2))
                elif name[0] in "QK":
                    t, pair = "QK".index(name[0]), int(name[1])
                    dst = (q_st, k_hh)[t]
                    if kind == PRO:
                        if name == "K0":
                            act.wait_ge(bias_scaled, 1)
                    else:
                        if pair == 0:
                            act.wait_ge(ring_full, at.base("ring_full") - ring_back(at, (("H", 1, 1), IT - 1, 0)))
                        else:
                            act.wait_ge(ring_full, at.of("ring_full", (("H", 3, 1), IT - 1, 0)))
                        copied, copies = ((q_moved, Q_COPIES), (k_dup, K_COPIES))[t]
                        act.wait_ge(copied[pair], (projections(kind, n) - 1) * copies * 16)
                    last = upper(dst[:, 2 * pair, :], src[:, :], bias=bias0[:, t, pair:pair + 1])
                elif name[0] == "V":
                    half = "ab".index(name[1])
                    if kind != PRO:
                        act.wait_ge(pv_done, at.of("pv_done", (("H", 2, 1), JT - 1)))
                    jt = slice(half * JT // 2, (half + 1) * JT // 2)
                    view = src[:, :].rearrange("p (j h d) -> p j h d", h=HEADS, d=D)
                    for h in range(HEADS - 1):
                        upper(v_st[:, h, jt, 0:D], view[:, :, h, :])
                    stage = x_stage[:, 0:JT * D].rearrange("p (j d) -> p j d", d=D)
                    if name == "Va":
                        act.wait_ge(split_lo, at.of("split_lo", "x1") if kind == PRO else at.base("split_lo"))
                    last = nc.scalar.activation(stage[:, jt, :], view[:, :, HEADS - 1, :], ACT.Identity)
                elif name[0] == "g":
                    last = upper(og_hi[:, int(name[1]), :], src[:, :])
                else:
                    half = "ab".index(name[1])
                    last = upper(v1_hi[:, half * JT // 2:(half + 1) * JT // 2, :],
                                 src[:, :].rearrange("p (j c) -> p j c", c=C))
                last.then_inc(hi_done, 1)

            def task(name):
                if name[0] in "xy":
                    cc = int(name[1])
                    if name == "y0":
                        act.wait_ge(ring_full, at.of("ring_full", "K1" if kind == PRO else
                                                     (L1_UNITS[1], IT - 1, 0)))
                    act.wait_ge(x_loaded, x_loads(kind, n, name))
                    upper(chan_hi[:, cc, :], x_stage[:, :]).then_inc(split_hi, 1)
                elif name == "VS":
                    if kind == BODY:
                        act.wait_ge(pv_done, at.of("pv_done", (("H", 3, 1), JT - 1)))
                    act.wait_ge(hi_done, at.of("hi_done", "Vb"))
                    upper(v_st[:, HEADS - 1, :, 0:D],
                          x_stage[:, 0:JT * D].rearrange("p (j d) -> p j d", d=D)).then_inc(split_hi, 1)
                elif name[0] == "O":
                    if name == "O0":
                        act.wait_ge(acc_done, at.base("acc_done") - acc_back(at, ("H", 1, 1)))
                        act.wait_ge(ring_full, at.base("ring_full"))
                    else:
                        act.wait_ge(acc_done, at.of("acc_done", ("H", 3, "ab".index(name[2]))))
                    pair, cols = attention_part(name)
                    upper(og_hi[:, pair, cols], o_f[:, pair, cols]).then_inc(split_hi, 1)
                elif name in ("h0", "h1"):
                    cc = int(name[1])
                    act.wait_ge(h_done, at.of("h_done", name))
                    if kind == BODY and cc == 0:
                        act.wait_ge(ring_full, at.of("ring_full", "K1"))
                    upper(chan_hi[:, cc, :], x_stage[:, :]).then_inc(split_hi, 1)

            def take_lower(u):
                layer, h, c = u
                if layer == "L":
                    return
                act.wait_ge(pv_done, at.of("pv_done", (u, JT - 1)))
                if h == 0 and c == 0:
                    act.wait_ge(q_moved[1], projections(kind, n) * Q_COPIES * 16)
                if h == 2 and c == 0 and kind == BODY:
                    act.wait_ge(split_lo, at.of("split_lo", "O1b"))
                nc.scalar.activation(o_f[D * (h % 2):D * (h % 2) + D, h // 2, c * HALF:(c + 1) * HALF],
                                     acc[c][D:2 * D, :], ACT.Identity).then_inc(acc_lower, 1)

            if kind == PRO:
                act.wait_ge(vec_loaded, 10 * 16)
                nc.scalar.activation(bias0[:, 0, :], bias0[:, 0, :], ACT.Copy, scale=Q_SCALE).then_inc(bias_scaled, 1)
            for s, sl in enumerate(slots):
                done = finished(slots, s)
                last_slot = s == len(slots) - 1
                for u in [] if last_slot else done:
                    take_lower(u)
                if sl["tile"]:
                    for u, jt in jts(slots, s):
                        i = ORDER["t_full"][kind].index((u, jt))
                        act.wait_ge(t_full, at.base("t_full") + i + 1)
                        if i >= 4 or kind != PRO:
                            act.wait_ge(pv_done, at.base("t_full") + i + 1 - 4)
                        upper(pt_hi[:, jt % 4, :], tbank[jt % 2][:, :]).then_inc(thi_done, 1)
                for u in done if last_slot else []:
                    take_lower(u)
                tile = norm_tile(kind, s)
                if tile and tile[1] not in POOL_NORM:
                    normalise(tile)
                tile = softmax_tile(kind, s)
                if tile:
                    exponent(tile)
                if sl["fill"] and sl["fill"] not in NO_HI:
                    fill_hi(sl["fill"])
                for name in stage_tasks(sl, kind, n):
                    task(name)

        def dve_part(dve, kind, n):
            at = At(kind, n)
            slots = SLOTS[kind]
            links = [0]

            def link(instruction):
                links[0] += 1
                instruction.then_inc(chain, 1)
                dve.wait_ge(chain, image_passes(kind, n) * CHAIN + links[0])

            def lower(dst, src, hi, scale=None, bias=None):
                if scale is None and bias is None:
                    return nc.vector.tensor_tensor(dst, src, hi.bitcast(F32), ALU.subtract)
                if bias is None:
                    return nc.vector.scalar_tensor_tensor(dst, src, scale, hi.bitcast(F32), ALU.mult, ALU.subtract)
                return nc.vector.scalar_tensor_tensor(dst, src, bias, hi.bitcast(F32), ALU.add, ALU.subtract)

            def fill_lo(name):
                src = ring[at.ring_buffer(name)]
                if name in NO_HI:
                    dve.wait_ge(ring_full, at.of("ring_full", name))
                else:
                    dve.wait_ge(hi_done, at.of("hi_done", name))
                if name in ("w0", "w1"):
                    cc = int(name[1])
                    lower(wp_lo[:, cc, 0, :], src[:, 0:C], wp_hi[:, cc, 0, :], scale=Q_SCALE)
                    last = lower(wp_lo[:, cc, 1:3, :], src[:, C:3 * C].rearrange("p (t c) -> p t c", t=2),
                                 wp_hi[:, cc, 1:3, :])
                elif name == "w2":
                    last = lower(wo_lo[:, :, :], src[:, 0:2 * C].rearrange("p (t c) -> p t c", t=2), wo_hi[:, :, :])
                elif name == "w3":
                    last = nc.vector.memset(mhalf[:, :], -0.5)
                elif name == "w4":
                    last = lower(a_lo[:, :, :], src[:, 0:2 * C].rearrange("p (t c) -> p t c", t=2), a_hi[:, :, :],
                                 scale=L1_SCALE)
                elif name == "w5":
                    last = lower(b_lo[:, :, :], src[:, 0:2 * C].rearrange("p (t c) -> p t c", t=2), b_hi[:, :, :])
                elif name[0] == "Q":
                    pair = int(name[1])
                    if pair == 1:
                        dve.wait_ge(q_moved[0], projections(kind, n) * Q_COPIES * 16)
                    elif kind == BODY:
                        dve.wait_ge(split_lo, at.of("split_lo", "O0"))
                    last = lower(o_f[:, 0, :], src[:, :], q_st[:, 2 * pair, :], bias=bias0[:, 0, pair:pair + 1])
                elif name[0] == "K":
                    pair = int(name[1])
                    last = lower(k_ll[:, 2 * pair, :], src[:, :], k_hh[:, 2 * pair, :], bias=bias0[:, 1, pair:pair + 1])
                elif name[0] == "V":
                    half = "ab".index(name[1])
                    jt = slice(half * JT // 2, (half + 1) * JT // 2)
                    view = src[:, :].rearrange("p (j h d) -> p j h d", h=HEADS, d=D)
                    for h in range(HEADS - 1):
                        last = lower(v_st[:, h, jt, D:2 * D], view[:, :, h, :], v_st[:, h, jt, 0:D])
                elif name[0] == "W":
                    m = int(name[1])
                    dve.wait_ge(resid_loaded, (image_passes(kind, n) + 1) * CC * 16)
                    last = nc.vector.scalar_tensor_tensor(resid[:, m, :], src[:, :], vecs[:, 0, m:m + 1],
                                                          resid[:, m, :], ALU.add, ALU.add)
                elif name[0] == "g":
                    last = lower(og_lo[:, int(name[1]), :], src[:, :], og_hi[:, int(name[1]), :])
                else:
                    half = "ab".index(name[1])
                    jt = slice(half * JT // 2, (half + 1) * JT // 2)
                    last = lower(v1_lo[:, jt, :], src[:, :].rearrange("p (j c) -> p j c", c=C), v1_hi[:, jt, :])
                last.then_inc(lo_done, 1)

            def take_stat(name):
                src = acc[0]
                dve.wait_ge(stat_full, at.of("stat_full", name))
                if name == "G2":
                    nc.vector.tensor_scalar(varp[:, :], src[:, 0:CC], EPS, None, ALU.add).then_inc(stat_taken, 1)
                    return
                nc.vector.tensor_copy(gm[:, :], src[:, 0:CC]).then_inc(stat_taken, 1)
                dve.wait_ge(stat_taken, at.of("stat_taken", "G1"))
                link(nc.vector.tensor_tensor(dev[:, :], mv[:, :, 0], gm[:, :], ALU.subtract))
                link(nc.vector.tensor_tensor(dev2[:, :], dev[:, :], dev[:, :], ALU.mult))
                nc.vector.tensor_tensor(spread[:, :], dev2[:, :], mv[:, :, 1], ALU.add).then_inc(dev_done, 1)

            def task(name):
                if name == "VS":
                    dve.wait_ge(split_hi, at.of("split_hi", "VS"))
                    stage = x_stage[:, 0:JT * D].rearrange("p (j d) -> p j d", d=D)
                    lower(v_st[:, HEADS - 1, :, D:2 * D], stage, v_st[:, HEADS - 1, :, 0:D]).then_inc(v3_lo, 1)
                elif name in ("s0", "s1"):
                    m = int(name[1])
                    dve.wait_ge(lo_done, at.of("lo_done", f"W{m}"))
                    nc.vector.bn_stats(bst[:, m, 0, :], resid[:, m, 0:HALF])
                    nc.vector.bn_stats(bst[:, m, 1, :], resid[:, m, HALF:HW])
                    dve.drain()
                    nc.vector.bn_aggr(mv[:, m, :], bst[:, m, :, :].rearrange("p a b -> p (a b)")).then_inc(stats_done, 1)
                elif name in ("h0", "h1"):
                    cc = int(name[1])
                    if cc == 0:
                        dve.wait_ge(rstd_done, at.of("rstd_done", "rstd"))
                        link(nc.vector.tensor_tensor(ga[:, :], rstd[:, :], vecs[:, 1, :], ALU.mult))
                        link(nc.vector.tensor_tensor(gam[:, :], gm[:, :], ga[:, :], ALU.mult))
                        link(nc.vector.tensor_tensor(gb[:, :], vecs[:, 2, :], gam[:, :], ALU.subtract))
                    else:
                        dve.wait_ge(split_lo, at.of("split_lo", "h0"))
                    nc.vector.tensor_scalar(x_stage[:, :], resid[:, cc, :], ga[:, cc:cc + 1], gb[:, cc:cc + 1],
                                            ALU.mult, ALU.add).then_inc(h_done, 1)

            def take_result(u):
                layer, h, c = u
                cols = slice(c * HALF, (c + 1) * HALF)
                if layer == "H":
                    dve.wait_ge(acc_lower, at.of("acc_lower", u))
                    rows = slice(D * (h % 2), D * (h % 2) + D)
                    o = o_f[rows, h // 2, cols]
                    nc.vector.scalar_tensor_tensor(o, acc[c][0:D, :], bias0[rows, 2, h // 2:h // 2 + 1], o,
                                                   ALU.add, ALU.add).then_inc(acc_done, 1)
                else:
                    dve.wait_ge(pv_done, at.of("pv_done", (u, JT - 1)))
                    for m in range(CC):
                        last = nc.vector.scalar_tensor_tensor(resid[:, m, cols], acc[m][:, :], vecs[:, 3, m:m + 1],
                                                              resid[:, m, cols], ALU.add, ALU.add)
                    last.then_inc(acc_done, 1)

            if kind == PRO:
                dve.wait_ge(vec_loaded, 10 * 16)
            for s, sl in enumerate(slots):
                tile = softmax_tile(kind, s)
                if tile:
                    b = buf(*tile[:2])
                    dve.wait_ge(ring_full, ring_value(at, tile))
                    nc.vector.tensor_reduce(negmax[:, b:b + 1], ring[ring_of(at, tile)][:, :], axis=AX.X, op=ALU.max,
                                            negate=True).then_inc(max_done, 1)
                tile = norm_tile(kind, s)
                if tile:
                    b = buf(*tile[:2])
                    dve.wait_ge(exp_done, at.of_tile("exp_done", tile))
                    nc.vector.reciprocal(rden[:, b:b + 1], den[:, b:b + 1]).then_inc(rden_done, 1)
                done = finished(slots, s)
                urgent = s + 1 < len(slots) and any(
                    slots[v]["tile"][0][0] == "L" for v in value_slots(slots, s + 1))
                for u in done if urgent else []:
                    take_result(u)
                if sl["tile"]:
                    for u, jt in jts(slots, s):
                        i = ORDER["t_full"][kind].index((u, jt))
                        dve.wait_ge(thi_done, at.base("t_full") + i + 1)
                        lower(pt_lo[:, jt % 4, :], tbank[jt % 2][:, :], pt_hi[:, jt % 4, :]).then_inc(tlo_done, 1)
                for u in [] if urgent else done:
                    take_result(u)
                if sl["stat"]:
                    take_stat(sl["stat"])
                if sl["fill"]:
                    fill_lo(sl["fill"])
                for name in stage_tasks(sl, kind, n):
                    task(name)

        def pool_part(pool, kind, n):
            at = At(kind, n)
            slots = SLOTS[kind]
            if kind == PRO:
                pool.memset(ident[:, :], 0.0).then_inc(const_made, 1)
                pool.memset(gmean[:, :], 1.0 / GSIZE).then_inc(const_made, 1)
                pool.wait_ge(const_made, 2)
                pool.affine_select(out=ident[:, :], in_=ident[:, :], compare_op=ALU.not_equal, fill=1.0, base=0,
                                   pattern=[[-1, P]], channel_multiplier=1).then_inc(const_made, 1)
                g = gmean[:, :].rearrange("p (g c) -> p g c", c=GSIZE)
                pool.affine_select(out=g, in_=g, compare_op=ALU.is_ge, fill=0.0, base=0,
                                   pattern=[[-GSIZE, P // GSIZE], [0, GSIZE]], channel_multiplier=1).then_inc(const_made, 1)
                pool.wait_ge(const_made, 4)
                pool.affine_select(out=g, in_=g, compare_op=ALU.is_ge, fill=0.0, base=GSIZE - 1,
                                   pattern=[[GSIZE, P // GSIZE], [0, GSIZE]], channel_multiplier=-1).then_inc(const_made, 1)
            for s, sl in enumerate(slots):
                tile = norm_tile(kind, s)
                if tile and tile[1] in POOL_NORM:
                    b = buf(*tile[:2])
                    pool.wait_ge(rden_done, at.of("rden_done", tile))
                    pool.tensor_tensor(probs[:, b, :], probs[:, b, :], rden[:, b:b + 1].to_broadcast([P, HW]), ALU.mult).then_inc(norm_pool, 1)
                if sl["stat"] == "G2":
                    pool.wait_ge(stat_taken, at.of("stat_taken", "G2"))
                    pool.tensor_tensor(rstd[:, :], varp[:, :], mhalf[:, :], ALU.pow).then_inc(rstd_done, 1)
                for name in stage_tasks(sl, kind, n):
                    if name[0] in "xyOh":
                        if name[0] == "O":
                            cc, cols = attention_part(name)
                            hi, lo, src = og_hi, og_lo, o_f[:, cc, cols]
                        else:
                            cc, cols = int(name[1]), slice(0, HW)
                            hi, lo, src = chan_hi, chan_lo, x_stage[:, :]
                        pool.wait_ge(split_hi, at.of("split_hi", name))
                        pool.tensor_tensor(lo[:, cc, cols], src, hi[:, cc, cols].bitcast(F32),
                                           ALU.subtract).then_inc(split_lo, 1)

        def ring_back(at, key):
            before = [BODY] if at.kind == LAST else [PRO, BODY]
            found = {len(ORDER["ring_full"][k]) - ORDER["ring_full"][k].index(key) - 1
                     for k in before if key in ORDER["ring_full"][k]}
            return min(found)

        def acc_back(at, unit):
            before = [BODY] if at.kind == LAST else [PRO, BODY]
            return min(len(ORDER["acc_done"][k]) - ORDER["acc_done"][k].index(unit) - 1 for k in before)

        def ring_value(at, tile):
            if tile in ORDER["ring_full"][at.kind]:
                return at.of("ring_full", tile)
            return at.of("ring_full", (tile[0], tile[1], 1), previous=True)

        def ring_of(at, tile):
            if tile in ORDER["ring_full"][at.kind]:
                return at.ring_buffer(tile)
            first = 0 if at.kind == PRO else len(ORDER["ring_full"][PRO])
            return (first - 1 - at.back("ring_full", (tile[0], tile[1], 1))) % 2

        def free_probs(act, at, tile):
            done = ORDER["t_full"][at.kind]
            u, it, gen = tile
            if gen == 1:
                units = [t[0] for t in (sl["tile"] for sl in SLOTS[at.kind]) if t and t[1] == 0]
                old = units[REST_UNITS.index(u) - 2]
                act.wait_ge(t_full, at.of("t_full", (old, JT - 1)))
                return
            units = [t[0] for t in (sl["tile"] for sl in SLOTS[at.kind]) if t and t[1] == 0]
            k = units.index(u) - 2
            if k >= 0:
                act.wait_ge(t_full, at.of("t_full", (units[k], JT - 1)))
            elif at.kind != PRO:
                act.wait_ge(t_full, at.base("t_full") + (k + 1) * JT)

        def whole(engine, part):
            part(engine, PRO, 0)
            with engine.Fori(0, LOOPS - 1) as n:
                part(engine, BODY, n)
            part(engine, BODY, LOOPS - 1)
            part(engine, LAST, B - 1)

        @block.sync
        def _(sp):
            whole(sp, sp_part)

        @block.gpsimd
        def _(pool):
            whole(pool, pool_part)

        @block.scalar
        def _(act):
            whole(act, act_part)

        @block.vector
        def _(dve):
            whole(dve, dve_part)

        @block.tensor
        def _(pe):
            whole(pe, pe_part)


_INS = ['x', 'L0_conv_Wp', 'L0_conv_bp', 'L0_conv_Wo', 'L0_conv_bo', 'L1_conv_norm_w', 'L1_conv_norm_b',
        'L1_conv_qkv_w', 'L1_conv_proj_w', 'L1_conv_proj_b']
_OUTS = [((B, C, 32, 32), 'float32')]


def kernel(**inputs):
    import numpy as _np
    import concourse.bacc as _bacc
    from concourse import mybir as _mybir
    from concourse.bass_utils import run_bass_kernel_spmd as _run

    nc = _bacc.Bacc("TRN2", target_bir_lowering=False, num_devices=1)
    arrays, args = {}, []
    for name in _INS:
        a = _np.ascontiguousarray(inputs[name])
        arrays[f"in_{name}_dram"] = a
        args.append(nc.dram_tensor(f"in_{name}_dram", a.shape, _mybir.dt.from_np(a.dtype), kind="ExternalInput").ap())
    for i, (shape, dtype) in enumerate(_OUTS):
        dt = _mybir.dt.from_np(_np.dtype(dtype))
        args.append(nc.dram_tensor(f"out_{i}_dram", shape, dt, kind="ExternalOutput").ap())
    build_program(nc, *args)
    r = _run(nc, [arrays], core_ids=[0])
    got = tuple(r.results[0][f"out_{i}_dram"] for i in range(len(_OUTS)))
    return got[0]
```

```python
import numpy as np
import concourse.bass as bass
import concourse.mybir as mybir
from contextlib import ExitStack

F32 = mybir.dt.float32
F32R = mybir.dt.float32r
ALU = mybir.AluOpType
ACT = mybir.ActivationFunctionType
AX = mybir.AxisListType

P = 128
B, C, HW = 16, 256, 32 * 32
HEADS, D = 4, 64
CC = C // P
JT = HW // P
HALF = 512
IT = HALF // P
GROUPS = 8
GSIZE = C // GROUPS
EPS = 1e-5
Q_SCALE = D ** -0.5
L1_SCALE = C ** -0.5
LEAD = 6
LAG = 2
POOL_NORM = (0, 1, 2)

PRO, BODY, LAST = "prologue", "body", "last"
LOOPS = B - 1



def heads(*hs):
    return [("H", h, c) for h in hs for c in range(2)]


L1_UNITS = [("L", 0, 1), ("L", 0, 0)]
REST_UNITS = [("H", 2, 1)] + heads(3)
NEXT_TILES = [(REST_UNITS[i // IT], i % IT) for i in range(LEAD)]


def tiles_of(units, gen):
    return [(u, it, gen) for u in units for it in range(IT)]


SCHEDULE = {
    PRO: (9 + LEAD, None,
        {0: "w0", 1: "w1", 2: "w2", 3: "K0", 4: "Q0", 5: "w3", 6: "w4", 7: "w5", 8: "Va", 9: "Vb", 14: "Q1", 16: "K1"},
        {},
        {0: ["x0", "x1"], 13: ["VS"], 20: ["y0"], 24: ["y1"], 33: ["O0"]}),
    BODY: (0, None,
        {0: "K0", 1: "Q0", 7: "Va", 9: "Vb", 15: "W0", 16: "W1", 18: "Q1", 19: "K1", 22: "g0", 23: "g1", 26: "va", 30: "vb"},
        {17: "G1", 19: "G2"},
        {9: ["O1a"], 13: ["O1b"], 15: ["VS"], 17: ["s0"], 18: ["s1"], 19: ["m0", "h0"], 20: ["m1", "h1"], 34: ["y0"], 37: ["y1"], 38: ["O0"]}),
    LAST: (0, (12, 14),
        {14: "W0", 15: "W1", 18: "g0", 19: "g1", 20: "va", 22: "vb"},
        {16: "G1", 17: "G2"},
        {10: ["O1a"], 13: ["O1b"], 16: ["s0", "s1"], 17: ["m0", "m1", "h0", "h1"]}),
}


def make_slots(kind):
    first_units = heads(0, 1) + [("H", 2, 0)]
    units = {PRO: first_units, BODY: REST_UNITS + first_units + L1_UNITS, LAST: REST_UNITS + L1_UNITS}[kind]
    lead_in, gap, fill, stat, do = SCHEDULE[kind]
    real = tiles_of(units, 0)
    order = [None] * lead_in + real
    if gap:
        order = order[:gap[0]] + [None] * gap[1] + order[gap[0]:]
    following = [] if kind == LAST else [(u, it, 1) for u, it in NEXT_TILES]
    slots = []
    for s, t in enumerate(order):
        a = s + LEAD
        ahead = order[a] if a < len(order) else (following[a - len(order)] if a - len(order) < len(following) else None)
        slots.append(dict(tile=t, score=ahead, fill=fill.get(s), stat=stat.get(s),
                          do=do.get(s, [])))
    return slots


SLOTS = {k: make_slots(k) for k in (PRO, BODY, LAST)}


def value_slots(slots, s):
    out = [s - LAG] if s >= LAG and slots[s - LAG]["tile"] else []
    if s == len(slots) - 1:
        out += [k for k in range(s - LAG + 1, s + 1) if slots[k]["tile"]]
    return out


def finished(slots, s):
    return [slots[k]["tile"][0] for k in value_slots(slots, s) if slots[k]["tile"][1] == IT - 1]




def ring_order(kind):
    out = []
    for sl in SLOTS[kind]:
        out += [sl["fill"]] if sl["fill"] else []
        out += [sl["score"]] if sl["score"] else []
    return out


def softmax_tile(kind, s):
    if s == 0:
        return None if kind == PRO else (*NEXT_TILES[-1], 0)
    return SLOTS[kind][s - 1]["score"]


def norm_tile(kind, s):
    if s == 0:
        return None if kind == PRO else (*NEXT_TILES[-2], 0)
    return softmax_tile(kind, s - 1)


def softmax_order(kind):
    return [t for t in (softmax_tile(kind, s) for s in range(len(SLOTS[kind]))) if t]


def norm_order(kind):
    return [t for t in (norm_tile(kind, s) for s in range(len(SLOTS[kind]))) if t]


def per_slot(kind, of):
    return [x for s in range(len(SLOTS[kind])) for x in of(SLOTS[kind], s)]


def jts(slots, k):
    u, it, _ = slots[k]["tile"]
    return [(u, 2 * it), (u, 2 * it + 1)]


def order_of(pick):
    return {k: pick(k) for k in (PRO, BODY, LAST)}


def done_fills(kind, skip=()):
    return [sl["fill"] for sl in SLOTS[kind] if sl["fill"] and sl["fill"] not in skip]


def tasks(kind, names):
    return [d for sl in SLOTS[kind] for d in sl["do"] if d in names]


NEXT_X = ("y0", "y1")
NO_HI = ("W0", "W1")

ORDER = {
    "ring_full": order_of(ring_order),
    "t_full": order_of(lambda k: per_slot(k, lambda sl, s: jts(sl, s) if sl[s]["tile"] else [])),
    "pv_done": order_of(lambda k: per_slot(k, lambda sl, s: [j for v in value_slots(sl, s) for j in jts(sl, v)])),
    "max_done": order_of(softmax_order),
    "exp_done": order_of(softmax_order),
    "rden_done": order_of(norm_order),
    "norm_act": order_of(lambda k: [t for t in norm_order(k) if t[1] not in POOL_NORM]),
    "norm_pool": order_of(lambda k: [t for t in norm_order(k) if t[1] in POOL_NORM]),
    "hi_done": order_of(lambda k: done_fills(k, NO_HI)),
    "lo_done": order_of(done_fills),
    "acc_lower": order_of(lambda k: [u for u in per_slot(k, finished) if u[0] == "H"]),
    "acc_done": order_of(lambda k: per_slot(k, finished)),
    "split_hi": order_of(lambda k: tasks(k, ("x0", "x1", "y0", "y1", "VS", "O0", "O1a", "O1b", "h0", "h1"))),
    "split_lo": order_of(lambda k: tasks(k, ("x0", "x1", "y0", "y1", "O0", "O1a", "O1b", "h0", "h1"))),
    "v3_lo": order_of(lambda k: tasks(k, ("VS",))),
    "h_done": order_of(lambda k: tasks(k, ("m0", "m1"))),
    "stats_done": order_of(lambda k: tasks(k, ("s0", "s1"))),
    "stat_full": order_of(lambda k: [sl["stat"] for sl in SLOTS[k] if sl["stat"]]),
    "stat_taken": order_of(lambda k: [sl["stat"] for sl in SLOTS[k] if sl["stat"]]),
    "affine_done": order_of(lambda k: ["affine"] if k != PRO else []),
}
assert len(ORDER["ring_full"][BODY]) % 2 == 0


class At:

    def __init__(self, kind, n):
        self.kind, self.n = kind, n

    def base(self, name):
        o = ORDER[name]
        if self.kind == PRO:
            return 0
        if self.kind == BODY:
            return self.n * len(o[BODY]) + len(o[PRO])
        return LOOPS * len(o[BODY]) + len(o[PRO]) - len([k for k in o[BODY] if k in NEXT_X])

    def back(self, name, key):
        before = [BODY] if self.kind == LAST else [PRO, BODY]
        found = {len(ORDER[name][k]) - ORDER[name][k].index(key) - 1 for k in before}
        assert len(found) == 1, (name, key, found)
        return found.pop()

    def of(self, name, key, previous=False):
        if previous:
            return self.base(name) - self.back(name, key)
        order = ORDER[name][self.kind]
        if self.kind == BODY and isinstance(self.n, int):
            order = [k for k in order if k not in NEXT_X]
        return self.base(name) + order.index(key) + 1

    def of_tile(self, name, tile):
        if tile in ORDER[name][self.kind]:
            return self.of(name, tile)
        return self.of(name, (tile[0], tile[1], 1), previous=True)

    def ring_buffer(self, key):
        first = 0 if self.kind == PRO else len(ORDER["ring_full"][PRO])
        return (first + ORDER["ring_full"][self.kind].index(key)) % 2


def build_program(nc, x, Wp, bp, Wo, bo, norm_w, norm_b, qkv_w, proj_w, proj_b, out):
    x_t = x.rearrange("b (cc p) h w -> b cc p (h w)", p=P)
    out_t = out.rearrange("b (cc p) h w -> b cc p (h w)", p=P)

    ctx = ExitStack()
    with ctx:
        def sb(name, shape, dt=F32):
            return ctx.enter_context(nc.sbuf_tensor(name, shape, dt))

        def sem(name):
            return ctx.enter_context(nc.semaphore(name))

        x_stage = sb("x_stage", [P, HW])
        resid = sb("resid", [P, CC, HW])
        chan_hi = sb("chan_hi", [P, CC, HW], F32R)
        chan_lo = sb("chan_lo", [P, CC, HW], F32R)
        q_st = sb("q_st", [P, HEADS, HW], F32R)
        k_hh = sb("k_hh", [P, HEADS, HW], F32R)
        k_ll = sb("k_ll", [P, HEADS, HW], F32R)
        v_st = sb("v_st", [P, HEADS, JT, 2 * D], F32R)
        probs = sb("probs", [P, 2 * IT, HW])
        pt_hi = sb("pt_hi", [P, 4, HALF], F32R)
        pt_lo = sb("pt_lo", [P, 4, HALF], F32R)
        o_f = sb("o_f", [P, CC, HW])
        og_hi = sb("og_hi", [P, CC, HW], F32R)
        og_lo = sb("og_lo", [P, CC, HW], F32R)
        v1_hi = sb("v1_hi", [P, JT, C], F32R)
        v1_lo = sb("v1_lo", [P, JT, C], F32R)
        wp_hi = sb("wp_hi", [P, CC, 3, C], F32R)
        wp_lo = sb("wp_lo", [P, CC, 3, C], F32R)
        wo_hi = sb("wo_hi", [P, CC, C], F32R)
        wo_lo = sb("wo_lo", [P, CC, C], F32R)
        a_hi = sb("a_hi", [P, CC, C], F32R)
        a_lo = sb("a_lo", [P, CC, C], F32R)
        b_hi = sb("b_hi", [P, CC, C], F32R)
        b_lo = sb("b_lo", [P, CC, C], F32R)
        bias0 = sb("bias0", [P, 3, CC])
        vecs = sb("vecs", [P, 4, CC])
        ident = sb("ident", [P, P])
        gmean = sb("gmean", [P, P])
        negmax = sb("negmax", [P, 2 * IT])
        den = sb("den", [P, 2 * IT])
        rden = sb("rden", [P, 2 * IT])
        csum = sb("csum", [P, CC])
        ngm = sb("ngm", [P, CC])
        spread = sb("spread", [P, CC])
        varp = sb("varp", [P, CC])
        mhalf = sb("mhalf", [P, CC])
        rstd = sb("rstd", [P, CC])
        ga = sb("ga", [P, CC])
        gam = sb("gam", [P, CC])
        gb = sb("gb", [P, CC])
        raw_wp = probs[:, 0:2, :].rearrange("p a (b c) -> p (a b) c", c=C)
        raw_wo = probs[:, 2, 0:2 * C].rearrange("p (a c) -> p a c", c=C)
        raw_pj = probs[:, 2, 2 * C:4 * C].rearrange("p (a c) -> p a c", c=C)
        raw_l1 = probs[:, 3:5, :].rearrange("p a (b c) -> p (a b) c", c=C)
        pj_t = probs[:, 5, 0:2 * C].rearrange("p (a c) -> p a c", c=C)

        ring = [ctx.enter_context(nc.psum_tensor(f"ring{i}", [P, HW], F32)) for i in range(2)]
        tbank = [ctx.enter_context(nc.psum_tensor(f"tbank{i}", [P, HALF], F32)) for i in range(2)]
        acc = [ctx.enter_context(nc.psum_tensor(f"acc{i}", [P, HALF], F32)) for i in range(2)]

        S = {name: sem(name) for name in ORDER}
        ring_full, t_full, pv_done = S["ring_full"], S["t_full"], S["pv_done"]
        max_done, exp_done, rden_done = S["max_done"], S["exp_done"], S["rden_done"]
        norm_act, norm_pool = S["norm_act"], S["norm_pool"]
        hi_done, lo_done, acc_lower, acc_done = S["hi_done"], S["lo_done"], S["acc_lower"], S["acc_done"]
        split_hi, split_lo, v3_lo, h_done = S["split_hi"], S["split_lo"], S["v3_lo"], S["h_done"]
        stat_full, stat_taken = S["stat_full"], S["stat_taken"]
        stats_done, affine_done = S["stats_done"], S["affine_done"]
        thi_done, tlo_done = sem("thi_done"), sem("tlo_done")
        chain = sem("chain")
        x_loaded, resid_loaded = sem("x_loaded"), sem("resid_loaded")
        k_dup = [sem("k_dup0"), sem("k_dup1")]
        q_moved = [sem("q_moved0"), sem("q_moved1")]
        stored = sem("stored")
        wp_loaded, w_loaded, vec_loaded, const_made, bias_scaled = sem("wp_loaded"), sem("w_loaded"), sem("vec_loaded"), sem("const_made"), sem("bias_scaled")
        K_COPIES, Q_COPIES = 6, 3
        CHAIN = 3

        block = ctx.enter_context(nc.Block())

        def buf(unit, it):
            return unit[2] * IT + it

        def final_pass(kind, n):
            return kind == BODY and isinstance(n, int)

        def stage_of(name):
            return o_f[:, 1, :] if name in ("x1", "h0") else x_stage[:, :]

        def lower_q(pair):
            return x_stage[:, :] if pair == 1 else o_f[:, 0, :]

        def stage_tasks(sl, kind, n):
            return [d for d in sl["do"] if not (final_pass(kind, n) and d in NEXT_X)]

        def attention_part(name):
            half = "ab".find(name[2:]) if name[2:] else None
            return int(name[1]), slice(0, HW) if half is None else slice(half * HALF, (half + 1) * HALF)

        def image_passes(kind, n):
            return 0 if kind == PRO else n if kind == BODY else LOOPS

        def x_loads(kind, n, name):
            if name[0] == "x":
                return 16 * CC
            image = 1 if kind == PRO else n + 2
            return 16 * (2 * image + int(name[1]) + 1)

        def projections(kind, n):
            return 1 if kind == PRO else n + 2

        def sp_part(sp, kind, n):
            at = At(kind, n)

            def load_x(image, cc):
                sp.dma_start(x_stage[:, :], x_t[image, cc]).then_inc(x_loaded, 16)

            low, high = slice(0, D), slice(D, 2 * D)

            def copy(dst, src, done):
                sp.dma_start(dst, src).then_inc(done, 16)

            def duplicate_k(pair):
                sp.wait_ge(lo_done, at.of("lo_done", f"K{pair}"))
                even, odd, done = 2 * pair, 2 * pair + 1, projections(kind, n) * K_COPIES * 16
                for k in (k_hh, k_ll):
                    for half in (low, high):
                        copy(k[half, odd, :].bitcast(F32), k[high, even, :].bitcast(F32), k_dup[pair])
                sp.wait_ge(k_dup[pair], done - 2 * 16)
                for k in (k_hh, k_ll):
                    copy(k[high, even, :].bitcast(F32), k[low, even, :].bitcast(F32), k_dup[pair])

            def stack_q(pair):
                lower = lower_q(pair)
                sp.wait_ge(lo_done, at.of("lo_done", f"Q{pair}"))
                even, odd, done = 2 * pair, 2 * pair + 1, projections(kind, n) * Q_COPIES * 16
                copy(q_st[low, odd, :].bitcast(F32), q_st[high, even, :].bitcast(F32), q_moved[pair])
                copy(q_st[high, odd, :].bitcast(F32), lower[high, :], q_moved[pair])
                sp.wait_ge(q_moved[pair], done - 16)
                copy(q_st[high, even, :].bitcast(F32), lower[low, :], q_moved[pair])

            def load_residual(image):
                sp.wait_ge(stored, (image * 4 + 1) * 16)
                for cc in range(CC):
                    sp.dma_start(resid[:, cc, :], x_t[image, cc]).then_inc(resid_loaded, 16)

            if kind == PRO:
                sp.sem_inc(stored, 16)
                wp_v = Wp.rearrange("(pr hh t d) c -> hh d t pr c", pr=2, hh=2, t=3)
                for hh in range(2):
                    for t in range(3):
                        sp.dma_start(raw_wp[D * hh:D * hh + D, 2 * t:2 * t + 2, :], wp_v[hh, :, t]).then_inc(wp_loaded, 16)
                for cc in range(CC):
                    sp.dma_start((x_stage[:, :], o_f[:, 1, :])[cc], x_t[0, cc]).then_inc(x_loaded, 16)
                bp_v = bp.rearrange("(pr hh t d) -> hh d t pr", pr=2, hh=2, t=3)
                for hh in range(2):
                    for t in range(3):
                        sp.dma_start(bias0[D * hh:D * hh + D, t, :], bp_v[hh, :, t],
                                     allow_slow_non_contiguous=True).then_inc(vec_loaded, 16)
                for i, v in enumerate((bo, norm_w, norm_b, proj_b)):
                    sp.dma_start(vecs[:, i, :], v.rearrange("(a p) -> p a", p=P),
                                 allow_slow_non_contiguous=True).then_inc(vec_loaded, 16)
                sp.dma_start(raw_wo, Wo.rearrange("(a p) c -> p a c", p=P)).then_inc(w_loaded, 16)
                sp.dma_start(raw_pj, proj_w.rearrange("(a p) c -> p a c", p=P)).then_inc(w_loaded, 16)
                sp.dma_start(raw_l1[:, 0:6, :], qkv_w.rearrange("(a p) c -> p a c", p=P)).then_inc(w_loaded, 16)
            if kind == LAST:
                load_residual(B - 1)
            else:
                duplicate_k(0)
                stack_q(0)
                if kind == BODY:
                    load_residual(n)
                stack_q(1)
                duplicate_k(1)
            if kind != LAST and not final_pass(kind, n):
                image = 1 if kind == PRO else n + 2
                if kind == PRO:
                    sp.wait_ge(q_moved[1], Q_COPIES * 16)
                else:
                    sp.wait_ge(split_lo, at.of("split_lo", "h1"))
                load_x(image, 0)
                sp.wait_ge(split_lo, at.of("split_lo", "y0"))
                load_x(image, 1)
            if kind != PRO:
                image = n if kind == BODY else B - 1
                for u in L1_UNITS:
                    sp.wait_ge(acc_done, at.of("acc_done", u))
                    cols = slice(u[2] * HALF, u[2] * HALF + HALF)
                    for cc in range(CC):
                        sp.dma_start(out_t[image, cc, :, cols], resid[:, cc, cols]).then_inc(stored, 16)
            if kind == LAST:
                sp.wait_ge(stored, (B * 4 + 1) * 16)

        def pe_part(pe, kind, n):
            at = At(kind, n)
            slots = SLOTS[kind]
            ring_keys = ORDER["ring_full"][kind]

            def products(dst, terms, start=True, stop=True):
                for i, (lhs, rhs) in enumerate(terms):
                    last = nc.tensor.matmul(dst, lhs, rhs, start=start and i == 0,
                                            stop=stop and i == len(terms) - 1)
                return last

            def take_ring(key):
                i = ring_keys.index(key)
                if i >= 2:
                    old, previous = ring_keys[i - 2], False
                elif kind == PRO:
                    return ring[at.ring_buffer(key)]
                else:
                    old, previous = ORDER["ring_full"][BODY][i - 2], True
                if isinstance(old, str):
                    pe.wait_ge(lo_done, at.of("lo_done", old))
                elif previous and old[:2] == NEXT_TILES[-1]:
                    pe.wait_ge(exp_done, at.of("exp_done", (*old[:2], 0)))
                else:
                    pe.wait_ge(exp_done, at.of("exp_done", old, previous))
                return ring[at.ring_buffer(key)]

            def scores(tile):
                (layer, h, c), it, gen = tile
                dst = take_ring(tile)
                q = slice((c * IT + it) * P, (c * IT + it + 1) * P)
                if layer == "H":
                    if c == 0 and it == 0 and h % 2 == 0:
                        pe.wait_ge(lo_done, at.of("lo_done", f"K{h // 2}"))
                        pe.wait_ge(k_dup[h // 2], projections(kind, n) * K_COPIES * 16)
                        pe.wait_ge(q_moved[h // 2], projections(kind, n) * Q_COPIES * 16)
                    for j in range(2):
                        keys = slice(j * HALF, (j + 1) * HALF)
                        last = products(dst[:, keys], [(q_st[:, h, q], k_hh[:, h, keys]),
                                                       (q_st[:, h, q], k_ll[:, h, keys])])
                else:
                    if tile[0] == L1_UNITS[0] and it == 0:
                        pe.wait_ge(lo_done, at.of("lo_done", "g1"))
                    for j in range(2):
                        keys = slice(j * HALF, (j + 1) * HALF)
                        last = products(dst[:, keys], [
                            (l[:, cc, q], r[:, cc, keys]) for cc in range(CC)
                            for l, r in ((og_hi, chan_hi), (og_hi, chan_lo), (og_lo, chan_hi))])
                last.then_inc(ring_full, 1)

            def by_channel(dst, w_hi, w_lo, a_h, a_l):
                for j in range(2):
                    cols = slice(j * HALF, (j + 1) * HALF)
                    last = products(dst[:, cols], [
                        (l[cc], r[:, cc, cols]) for cc in range(CC)
                        for l, r in ((w_hi, a_h), (w_hi, a_l), (w_lo, a_h))])
                return last

            def by_token(dst, half, w_hi, w_lo):
                for t in range(JT // 2):
                    tok = slice((half * JT // 2 + t) * P, (half * JT // 2 + t + 1) * P)
                    last = products(dst[:, t * C:(t + 1) * C], [
                        (l[:, cc, tok], r[cc]) for cc in range(CC)
                        for l, r in ((chan_hi, w_hi), (chan_hi, w_lo), (chan_lo, w_hi))])
                return last

            def filler(name):
                dst = take_ring(name)
                if name in ("w0", "w1"):
                    if name == "w0":
                        pe.wait_ge(wp_loaded, 6 * 16)
                        pe.wait_ge(const_made, 5)
                    cc = int(name[1])
                    for t in range(6):
                        last = nc.tensor.transpose(dst[:, t * P:(t + 1) * P], raw_wp[:, t, cc * P:(cc + 1) * P], ident[:, :])
                elif name in ("w2", "w3"):
                    if name == "w2":
                        pe.wait_ge(w_loaded, 3 * 16)
                    raw = raw_wo if name == "w2" else raw_pj
                    for cc in range(CC):
                        for a in range(2):
                            last = nc.tensor.transpose(dst[:, cc * C + a * P:cc * C + (a + 1) * P],
                                                       raw[:, a, cc * P:(cc + 1) * P], ident[:, :])
                elif name == "w4":
                    for m in range(CC):
                        last = products(dst[:, m * C:(m + 1) * C], [
                            (raw_l1[:, a, m * P:(m + 1) * P], raw_l1[:, 2 + a, :]) for a in range(2)])
                elif name == "w5":
                    pe.wait_ge(lo_done, at.of("lo_done", "w3"))
                    for m in range(CC):
                        last = products(dst[:, m * C:(m + 1) * C], [
                            (raw_l1[:, 4 + a, m * P:(m + 1) * P], pj_t[:, a, :]) for a in range(2)])
                elif name[0] in "QK":
                    t, pair = "QK".index(name[0]), int(name[1])
                    if kind == PRO:
                        pe.wait_ge(lo_done, at.of("lo_done", "w1"))
                        pe.wait_ge(split_hi, at.of("split_hi", "x1"))
                        pe.wait_ge(split_lo, at.of("split_lo", "x1"))
                    elif name == "K0":
                        pe.wait_ge(split_hi, at.base("split_hi"))
                        pe.wait_ge(split_lo, at.base("split_lo"))
                    cols = slice(pair * P, (pair + 1) * P)
                    last = by_channel(dst, [wp_hi[:, cc, t, cols] for cc in range(CC)],
                                      [wp_lo[:, cc, t, cols] for cc in range(CC)], chan_hi, chan_lo)
                elif name[0] == "V":
                    last = by_token(dst, "ab".index(name[1]), [wp_hi[:, cc, 2, :] for cc in range(CC)],
                                    [wp_lo[:, cc, 2, :] for cc in range(CC)])
                elif name[0] == "W":
                    pe.wait_ge(split_hi, at.of("split_hi", "O1b"))
                    pe.wait_ge(split_lo, at.of("split_lo", "O1b"))
                    cols = slice(int(name[1]) * P, (int(name[1]) + 1) * P)
                    last = by_channel(dst, [wo_hi[:, cc, cols] for cc in range(CC)],
                                      [wo_lo[:, cc, cols] for cc in range(CC)], og_hi, og_lo)
                elif name[0] == "g":
                    pe.wait_ge(split_hi, at.of("split_hi", "h1"))
                    pe.wait_ge(split_lo, at.of("split_lo", "h1"))
                    cols = slice(int(name[1]) * P, (int(name[1]) + 1) * P)
                    last = by_channel(dst, [a_hi[:, cc, cols] for cc in range(CC)],
                                      [a_lo[:, cc, cols] for cc in range(CC)], chan_hi, chan_lo)
                else:
                    last = by_token(dst, "ab".index(name[1]), [b_hi[:, cc, :] for cc in range(CC)],
                                    [b_lo[:, cc, :] for cc in range(CC)])
                last.then_inc(ring_full, 1)

            def stat(name):
                if name == "G1":
                    pe.wait_ge(lo_done, at.of("lo_done", "W1"))
                    pe.wait_ge(acc_done, at.of("acc_done", ("H", 3, 1)))
                    moving = csum[:, :]
                else:
                    if kind == BODY:
                        pe.wait_ge(acc_done, at.of("acc_done", ("H", 0, 0)))
                    pe.wait_ge(stats_done, at.of("stats_done", "s1"))
                    moving = spread[:, :]
                products(acc[1 if name == "G1" else 0][:, 0:CC], [(gmean[:, :], moving)]).then_inc(stat_full, 1)

            def transposes(s):
                u, it, _ = slots[s]["tile"]
                if it == 0:
                    pe.wait_ge(norm_act, at.of_tile("norm_act", (u, IT - 1, 0)))
                    pe.wait_ge(norm_pool, at.of_tile("norm_pool", (u, max(POOL_NORM), 0)))
                for u, jt in jts(slots, s):
                    i = ORDER["t_full"][kind].index((u, jt))
                    if i >= 2 or kind != PRO:
                        pe.wait_ge(tlo_done, at.base("t_full") + i - 1)
                    for q in range(IT):
                        last = nc.tensor.transpose(tbank[jt % 2][:, q * P:(q + 1) * P],
                                                   probs[:, buf(u, q), jt * P:(jt + 1) * P], ident[:, :])
                    last.then_inc(t_full, 1)

            def values(s):
                order = ORDER["acc_done"][kind]
                for u, jt in jts(slots, s):
                    i = ORDER["t_full"][kind].index((u, jt))
                    first, final = jt == 0, jt == JT - 1
                    if first:
                        k = order.index(u)
                        if u[0] == "L":
                            pe.wait_ge(acc_done, at.base("acc_done") + k)
                        elif kind != PRO and k < 2:
                            pe.wait_ge(acc_done, at.base("acc_done"))
                        elif k >= 2:
                            pe.wait_ge(acc_done, at.base("acc_done") + k - 1)
                        if u == ("H", 0, 0):
                            pe.wait_ge(lo_done, at.of("lo_done", "Vb"))
                        if u == ("H", 0, 1) and kind == BODY:
                            pe.wait_ge(stat_taken, at.of("stat_taken", "G1"))
                        if u == ("H", 1, 0) and kind == BODY or u == L1_UNITS[0] and kind == LAST:
                            pe.wait_ge(stat_taken, at.of("stat_taken", "G2"))
                        if u == ("H", 3, 0):
                            pe.wait_ge(v3_lo, at.base("v3_lo"))
                        if u == L1_UNITS[0]:
                            pe.wait_ge(lo_done, at.of("lo_done", "vb"))
                    pe.wait_ge(thi_done, at.base("t_full") + i + 1)
                    hi, lo = pt_hi[:, jt % 4, :], pt_lo[:, jt % 4, :]
                    if u[0] == "H":
                        v = v_st[:, u[1], jt, :]
                        nc.tensor.matmul(acc[u[2]][:, :], v, hi, start=first, stop=False)
                        pe.wait_ge(tlo_done, at.base("t_full") + i + 1)
                        last = nc.tensor.matmul(acc[u[2]][:, :], v, lo, start=False, stop=final)
                    else:
                        for m in range(CC):
                            o = slice(m * P, (m + 1) * P)
                            products(acc[m][:, :], [(v1_hi[:, jt, o], hi), (v1_lo[:, jt, o], hi)],
                                     start=first, stop=False)
                        pe.wait_ge(tlo_done, at.base("t_full") + i + 1)
                        for m in range(CC):
                            o = slice(m * P, (m + 1) * P)
                            last = products(acc[m][:, :], [(v1_hi[:, jt, o], lo)], start=False, stop=final)
                    last.then_inc(pv_done, 1)

            for s, sl in enumerate(slots):
                todo = value_slots(slots, s)
                if todo[:1] == [s - LAG]:
                    values(s - LAG)
                if sl["stat"]:
                    stat(sl["stat"])
                if sl["tile"]:
                    transposes(s)
                rest = [v for v in todo if v != s - LAG]
                for v in rest[:-1]:
                    values(v)
                if sl["fill"]:
                    filler(sl["fill"])
                if sl["score"]:
                    scores(sl["score"])
                for v in rest[-1:]:
                    values(v)

        def act_part(act, kind, n):
            at = At(kind, n)
            slots = SLOTS[kind]

            def upper(dst, src, **kw):
                return nc.scalar.activation(dst, src, ACT.Identity, **kw)

            def exponent(tile):
                u, it, _ = tile
                act.wait_ge(max_done, at.of("max_done", tile))
                free_probs(act, at, tile)
                b = buf(u, it)
                nc.scalar.activation(probs[:, b, :], ring[ring_of(at, tile)][:, :], ACT.Exp, bias=negmax[:, b:b + 1],
                                     accum_out=den[:, b:b + 1]).then_inc(exp_done, 1)

            def normalise(tile):
                b = buf(*tile[:2])
                act.wait_ge(rden_done, at.of("rden_done", tile))
                nc.scalar.activation(probs[:, b, :], probs[:, b, :], ACT.Copy,
                                     scale=rden[:, b:b + 1]).then_inc(norm_act, 1)

            def fill_hi(name):
                src = ring[at.ring_buffer(name)]
                act.wait_ge(ring_full, at.of("ring_full", name))
                if name in ("w0", "w1"):
                    cc = int(name[1])
                    upper(wp_hi[:, cc, 0, :], src[:, 0:C], scale=Q_SCALE)
                    last = upper(wp_hi[:, cc, 1:3, :], src[:, C:3 * C].rearrange("p (t c) -> p t c", t=2))
                elif name == "w2":
                    last = upper(wo_hi[:, :, :], src[:, 0:2 * C].rearrange("p (t c) -> p t c", t=2))
                elif name == "w3":
                    last = upper(pj_t, src[:, 0:2 * C].rearrange("p (t c) -> p t c", t=2))
                elif name == "w4":
                    last = upper(a_hi[:, :, :], src[:, 0:2 * C].rearrange("p (t c) -> p t c", t=2), scale=L1_SCALE)
                elif name == "w5":
                    last = upper(b_hi[:, :, :], src[:, 0:2 * C].rearrange("p (t c) -> p t c", t=2))
                elif name[0] in "QK":
                    t, pair = "QK".index(name[0]), int(name[1])
                    dst = (q_st, k_hh)[t]
                    if kind == PRO:
                        if name == "K0":
                            act.wait_ge(vec_loaded, 10 * 16)
                            nc.scalar.activation(bias0[:, 0, :], bias0[:, 0, :], ACT.Copy,
                                                 scale=Q_SCALE).then_inc(bias_scaled, 1)
                        elif name == "Q0":
                            act.wait_ge(bias_scaled, 1)
                    else:
                        if pair == 0:
                            act.wait_ge(ring_full, at.base("ring_full") - ring_back(at, (("H", 1, 1), IT - 1, 0)))
                        else:
                            act.wait_ge(ring_full, at.of("ring_full", (("H", 3, 1), IT - 1, 0)))
                        copied, copies = ((q_moved, Q_COPIES), (k_dup, K_COPIES))[t]
                        act.wait_ge(copied[pair], (projections(kind, n) - 1) * copies * 16)
                    last = upper(dst[:, 2 * pair, :], src[:, :], bias=bias0[:, t, pair:pair + 1])
                elif name[0] == "V":
                    half = "ab".index(name[1])
                    if kind != PRO:
                        act.wait_ge(pv_done, at.of("pv_done", (("H", 2, 1), JT - 1)))
                    jt = slice(half * JT // 2, (half + 1) * JT // 2)
                    view = src[:, :].rearrange("p (j h d) -> p j h d", h=HEADS, d=D)
                    for h in range(HEADS - 1):
                        upper(v_st[:, h, jt, 0:D], view[:, :, h, :])
                    stage = x_stage[:, 0:JT * D].rearrange("p (j d) -> p j d", d=D)
                    if name == "Va":
                        act.wait_ge(split_lo, at.of("split_lo", "x1") if kind == PRO else at.base("split_lo"))
                    last = nc.scalar.activation(stage[:, jt, :], view[:, :, HEADS - 1, :], ACT.Identity)
                elif name[0] == "g":
                    last = upper(og_hi[:, int(name[1]), :], src[:, :])
                else:
                    half = "ab".index(name[1])
                    last = upper(v1_hi[:, half * JT // 2:(half + 1) * JT // 2, :],
                                 src[:, :].rearrange("p (j c) -> p j c", c=C))
                last.then_inc(hi_done, 1)

            def task(name):
                if name[0] in "xy":
                    cc = int(name[1])
                    if name == "y0":
                        act.wait_ge(ring_full, at.of("ring_full", "K1" if kind == PRO else
                                                     (L1_UNITS[1], IT - 1, 0)))
                    act.wait_ge(x_loaded, x_loads(kind, n, name))
                    upper(chan_hi[:, cc, :], stage_of(name)).then_inc(split_hi, 1)
                elif name == "VS":
                    if kind == BODY:
                        act.wait_ge(pv_done, at.of("pv_done", (("H", 3, 1), JT - 1)))
                    act.wait_ge(hi_done, at.of("hi_done", "Vb"))
                    upper(v_st[:, HEADS - 1, :, 0:D],
                          x_stage[:, 0:JT * D].rearrange("p (j d) -> p j d", d=D)).then_inc(split_hi, 1)
                elif name[0] == "O":
                    if name == "O0":
                        act.wait_ge(acc_done, at.of("acc_done", ("H", 1, 1)))
                        if kind == BODY:
                            act.wait_ge(ring_full, at.of("ring_full", (L1_UNITS[1], IT - 1, 0)))
                    else:
                        act.wait_ge(acc_done, at.of("acc_done", ("H", 3, "ab".index(name[2]))))
                    pair, cols = attention_part(name)
                    upper(og_hi[:, pair, cols], o_f[:, pair, cols]).then_inc(split_hi, 1)
                elif name in ("s0", "s1"):
                    m = int(name[1])
                    act.wait_ge(stat_taken, at.of("stat_taken", "G1"))
                    if m == 1:
                        act.wait_ge(stats_done, at.of("stats_done", "s0"))
                    nc.scalar.activation(o_f[:, 1, :], resid[:, m, :], ACT.Square, bias=ngm[:, m:m + 1],
                                         accum_out=spread[:, m:m + 1]).then_inc(stats_done, 1)
                elif name in ("h0", "h1"):
                    cc = int(name[1])
                    act.wait_ge(h_done, at.of("h_done", f"m{cc}"))
                    if kind == BODY and cc == 0:
                        act.wait_ge(ring_full, at.of("ring_full", "K1"))
                    upper(chan_hi[:, cc, :], stage_of(name)).then_inc(split_hi, 1)

            def take_lower(u):
                layer, h, c = u
                if layer == "L":
                    return
                act.wait_ge(pv_done, at.of("pv_done", (u, JT - 1)))
                if h == 0 and c == 0:
                    act.wait_ge(q_moved[0], projections(kind, n) * Q_COPIES * 16)
                if h == 2 and c == 0 and kind == BODY:
                    act.wait_ge(split_lo, at.of("split_lo", "h1"))
                nc.scalar.activation(o_f[D * (h % 2):D * (h % 2) + D, h // 2, c * HALF:(c + 1) * HALF],
                                     acc[c][D:2 * D, :], ACT.Identity).then_inc(acc_lower, 1)

            for s, sl in enumerate(slots):
                done = finished(slots, s)
                last_slot = s == len(slots) - 1
                for u in [] if last_slot else done:
                    take_lower(u)
                if sl["tile"]:
                    for u, jt in jts(slots, s):
                        i = ORDER["t_full"][kind].index((u, jt))
                        act.wait_ge(t_full, at.base("t_full") + i + 1)
                        if i >= 4 or kind != PRO:
                            act.wait_ge(pv_done, at.base("t_full") + i + 1 - 4)
                        upper(pt_hi[:, jt % 4, :], tbank[jt % 2][:, :]).then_inc(thi_done, 1)
                for u in done if last_slot else []:
                    take_lower(u)
                tile = norm_tile(kind, s)
                if tile and tile[1] not in POOL_NORM:
                    normalise(tile)
                tile = softmax_tile(kind, s)
                if tile:
                    exponent(tile)
                if sl["fill"] and sl["fill"] not in NO_HI:
                    fill_hi(sl["fill"])
                for name in stage_tasks(sl, kind, n):
                    task(name)

        def dve_part(dve, kind, n):
            at = At(kind, n)
            slots = SLOTS[kind]

            def lower(dst, src, hi, scale=None, bias=None):
                if scale is None and bias is None:
                    return nc.vector.tensor_tensor(dst, src, hi.bitcast(F32), ALU.subtract)
                if bias is None:
                    return nc.vector.scalar_tensor_tensor(dst, src, scale, hi.bitcast(F32), ALU.mult, ALU.subtract)
                return nc.vector.scalar_tensor_tensor(dst, src, bias, hi.bitcast(F32), ALU.add, ALU.subtract)

            def fill_lo(name):
                src = ring[at.ring_buffer(name)]
                if name in NO_HI:
                    dve.wait_ge(ring_full, at.of("ring_full", name))
                else:
                    dve.wait_ge(hi_done, at.of("hi_done", name))
                if name in ("w0", "w1"):
                    cc = int(name[1])
                    lower(wp_lo[:, cc, 0, :], src[:, 0:C], wp_hi[:, cc, 0, :], scale=Q_SCALE)
                    last = lower(wp_lo[:, cc, 1:3, :], src[:, C:3 * C].rearrange("p (t c) -> p t c", t=2),
                                 wp_hi[:, cc, 1:3, :])
                elif name == "w2":
                    last = lower(wo_lo[:, :, :], src[:, 0:2 * C].rearrange("p (t c) -> p t c", t=2), wo_hi[:, :, :])
                elif name == "w3":
                    last = nc.vector.memset(mhalf[:, :], -0.5)
                elif name == "w4":
                    last = lower(a_lo[:, :, :], src[:, 0:2 * C].rearrange("p (t c) -> p t c", t=2), a_hi[:, :, :],
                                 scale=L1_SCALE)
                elif name == "w5":
                    last = lower(b_lo[:, :, :], src[:, 0:2 * C].rearrange("p (t c) -> p t c", t=2), b_hi[:, :, :])
                elif name[0] == "Q":
                    pair = int(name[1])
                    if pair == 1:
                        dve.wait_ge(v3_lo, at.of("v3_lo", "VS"))
                    elif kind == BODY:
                        dve.wait_ge(split_lo, at.base("split_lo"))
                    last = lower(lower_q(pair), src[:, :], q_st[:, 2 * pair, :], bias=bias0[:, 0, pair:pair + 1])
                elif name[0] == "K":
                    pair = int(name[1])
                    if kind == PRO and pair == 0:
                        dve.wait_ge(vec_loaded, 10 * 16)
                    last = lower(k_ll[:, 2 * pair, :], src[:, :], k_hh[:, 2 * pair, :], bias=bias0[:, 1, pair:pair + 1])
                elif name[0] == "V":
                    half = "ab".index(name[1])
                    jt = slice(half * JT // 2, (half + 1) * JT // 2)
                    view = src[:, :].rearrange("p (j h d) -> p j h d", h=HEADS, d=D)
                    for h in range(HEADS - 1):
                        last = lower(v_st[:, h, jt, D:2 * D], view[:, :, h, :], v_st[:, h, jt, 0:D])
                elif name[0] == "W":
                    m = int(name[1])
                    dve.wait_ge(resid_loaded, (image_passes(kind, n) + 1) * CC * 16)
                    last = nc.vector.scalar_tensor_tensor(resid[:, m, :], src[:, :], vecs[:, 0, m:m + 1],
                                                          resid[:, m, :], ALU.add, ALU.add,
                                                          accum_out=csum[:, m:m + 1])
                elif name[0] == "g":
                    last = lower(og_lo[:, int(name[1]), :], src[:, :], og_hi[:, int(name[1]), :])
                else:
                    half = "ab".index(name[1])
                    jt = slice(half * JT // 2, (half + 1) * JT // 2)
                    last = lower(v1_lo[:, jt, :], src[:, :].rearrange("p (j c) -> p j c", c=C), v1_hi[:, jt, :])
                last.then_inc(lo_done, 1)

            def take_stat(name):
                src = acc[1 if name == "G1" else 0]
                dve.wait_ge(stat_full, at.of("stat_full", name))
                if name == "G1":
                    nc.vector.tensor_scalar(ngm[:, :], src[:, 0:CC], -1.0, None, ALU.mult).then_inc(stat_taken, 1)
                else:
                    nc.vector.tensor_scalar(varp[:, :], src[:, 0:CC], EPS, None, ALU.add).then_inc(stat_taken, 1)

            def task(name):
                if name == "VS":
                    dve.wait_ge(split_hi, at.of("split_hi", "VS"))
                    stage = x_stage[:, 0:JT * D].rearrange("p (j d) -> p j d", d=D)
                    lower(v_st[:, HEADS - 1, :, D:2 * D], stage, v_st[:, HEADS - 1, :, 0:D]).then_inc(v3_lo, 1)
                elif name in ("m0", "m1"):
                    cc = int(name[1])
                    if cc == 1:
                        if kind == BODY:
                            dve.wait_ge(q_moved[1], projections(kind, n) * Q_COPIES * 16)
                    else:
                        dve.wait_ge(affine_done, at.of("affine_done", "affine"))
                    nc.vector.tensor_scalar(stage_of(f"h{cc}"), resid[:, cc, :], ga[:, cc:cc + 1], gb[:, cc:cc + 1],
                                            ALU.mult, ALU.add).then_inc(h_done, 1)

            def take_result(u):
                layer, h, c = u
                cols = slice(c * HALF, (c + 1) * HALF)
                if layer == "H":
                    dve.wait_ge(acc_lower, at.of("acc_lower", u))
                    rows = slice(D * (h % 2), D * (h % 2) + D)
                    o = o_f[rows, h // 2, cols]
                    nc.vector.scalar_tensor_tensor(o, acc[c][0:D, :], bias0[rows, 2, h // 2:h // 2 + 1], o,
                                                   ALU.add, ALU.add).then_inc(acc_done, 1)
                else:
                    dve.wait_ge(pv_done, at.of("pv_done", (u, JT - 1)))
                    for m in range(CC):
                        last = nc.vector.scalar_tensor_tensor(resid[:, m, cols], acc[m][:, :], vecs[:, 3, m:m + 1],
                                                              resid[:, m, cols], ALU.add, ALU.add)
                    last.then_inc(acc_done, 1)

            for s, sl in enumerate(slots):
                tile = softmax_tile(kind, s)
                if tile:
                    b = buf(*tile[:2])
                    dve.wait_ge(ring_full, ring_value(at, tile))
                    nc.vector.tensor_reduce(negmax[:, b:b + 1], ring[ring_of(at, tile)][:, :], axis=AX.X, op=ALU.max,
                                            negate=True).then_inc(max_done, 1)
                tile = norm_tile(kind, s)
                if tile:
                    b = buf(*tile[:2])
                    dve.wait_ge(exp_done, at.of_tile("exp_done", tile))
                    nc.vector.reciprocal(rden[:, b:b + 1], den[:, b:b + 1]).then_inc(rden_done, 1)
                done = finished(slots, s)
                urgent = s + 1 < len(slots) and any(
                    slots[v]["tile"][0][0] == "L" for v in value_slots(slots, s + 1)) or ("H", 3, 1) in done
                for u in done if urgent else []:
                    take_result(u)
                if sl["stat"]:
                    take_stat(sl["stat"])
                if sl["tile"]:
                    for u, jt in jts(slots, s):
                        i = ORDER["t_full"][kind].index((u, jt))
                        dve.wait_ge(thi_done, at.base("t_full") + i + 1)
                        lower(pt_lo[:, jt % 4, :], tbank[jt % 2][:, :], pt_hi[:, jt % 4, :]).then_inc(tlo_done, 1)
                for u in [] if urgent else done:
                    take_result(u)
                if sl["fill"]:
                    fill_lo(sl["fill"])
                for name in stage_tasks(sl, kind, n):
                    task(name)

        def pool_part(pool, kind, n):
            at = At(kind, n)
            slots = SLOTS[kind]
            if kind == PRO:
                pool.memset(ident[:, :], 0.0).then_inc(const_made, 1)
                pool.memset(gmean[:, :], 1.0 / (GSIZE * HW)).then_inc(const_made, 1)
                pool.wait_ge(const_made, 2)
                pool.affine_select(out=ident[:, :], in_=ident[:, :], compare_op=ALU.not_equal, fill=1.0, base=0,
                                   pattern=[[-1, P]], channel_multiplier=1).then_inc(const_made, 1)
                g = gmean[:, :].rearrange("p (g c) -> p g c", c=GSIZE)
                pool.affine_select(out=g, in_=g, compare_op=ALU.is_ge, fill=0.0, base=0,
                                   pattern=[[-GSIZE, P // GSIZE], [0, GSIZE]], channel_multiplier=1).then_inc(const_made, 1)
                pool.wait_ge(const_made, 4)
                pool.affine_select(out=g, in_=g, compare_op=ALU.is_ge, fill=0.0, base=GSIZE - 1,
                                   pattern=[[GSIZE, P // GSIZE], [0, GSIZE]], channel_multiplier=-1).then_inc(const_made, 1)
            for s, sl in enumerate(slots):
                tile = norm_tile(kind, s)
                if tile and tile[1] in POOL_NORM:
                    b = buf(*tile[:2])
                    pool.wait_ge(rden_done, at.of("rden_done", tile))
                    pool.tensor_tensor(probs[:, b, :], probs[:, b, :], rden[:, b:b + 1].to_broadcast([P, HW]), ALU.mult).then_inc(norm_pool, 1)
                if sl["stat"] == "G2":
                    steps = [(rstd, varp, mhalf, ALU.pow), (ga, rstd, vecs[:, 1, :], ALU.mult),
                             (gam, ngm, ga, ALU.mult), (gb, vecs[:, 2, :], gam, ALU.add)]
                    pool.wait_ge(stat_taken, at.of("stat_taken", "G2"))
                    for i, (dst, a, b, op) in enumerate(steps):
                        if i:
                            pool.wait_ge(chain, image_passes(kind, n) * CHAIN + i)
                        pool.tensor_tensor(dst[:, :], a[:, :], b[:, :], op).then_inc(
                            chain if i < CHAIN else affine_done, 1)
                for name in stage_tasks(sl, kind, n):
                    if name[0] in "xyOh":
                        if name[0] == "O":
                            cc, cols = attention_part(name)
                            hi, lo, src = og_hi, og_lo, o_f[:, cc, cols]
                        else:
                            cc, cols = int(name[1]), slice(0, HW)
                            hi, lo, src = chan_hi, chan_lo, stage_of(name)
                        pool.wait_ge(split_hi, at.of("split_hi", name))
                        pool.tensor_tensor(lo[:, cc, cols], src, hi[:, cc, cols].bitcast(F32),
                                           ALU.subtract).then_inc(split_lo, 1)

        def ring_back(at, key):
            before = [BODY] if at.kind == LAST else [PRO, BODY]
            found = {len(ORDER["ring_full"][k]) - ORDER["ring_full"][k].index(key) - 1
                     for k in before if key in ORDER["ring_full"][k]}
            return min(found)

        def ring_value(at, tile):
            if tile in ORDER["ring_full"][at.kind]:
                return at.of("ring_full", tile)
            return at.of("ring_full", (tile[0], tile[1], 1), previous=True)

        def ring_of(at, tile):
            if tile in ORDER["ring_full"][at.kind]:
                return at.ring_buffer(tile)
            first = 0 if at.kind == PRO else len(ORDER["ring_full"][PRO])
            return (first - 1 - at.back("ring_full", (tile[0], tile[1], 1))) % 2

        def free_probs(act, at, tile):
            done = ORDER["t_full"][at.kind]
            u, it, gen = tile
            if gen == 1:
                units = [t[0] for t in (sl["tile"] for sl in SLOTS[at.kind]) if t and t[1] == 0]
                old = units[REST_UNITS.index(u) - 2]
                act.wait_ge(t_full, at.of("t_full", (old, JT - 1)))
                return
            units = [t[0] for t in (sl["tile"] for sl in SLOTS[at.kind]) if t and t[1] == 0]
            k = units.index(u) - 2
            if k >= 0:
                act.wait_ge(t_full, at.of("t_full", (units[k], JT - 1)))
            elif at.kind != PRO:
                act.wait_ge(t_full, at.base("t_full") + (k + 1) * JT)

        def whole(engine, part):
            part(engine, PRO, 0)
            with engine.Fori(0, LOOPS - 1) as n:
                part(engine, BODY, n)
            part(engine, BODY, LOOPS - 1)
            part(engine, LAST, B - 1)

        @block.sync
        def _(sp):
            whole(sp, sp_part)

        @block.gpsimd
        def _(pool):
            whole(pool, pool_part)

        @block.scalar
        def _(act):
            whole(act, act_part)

        @block.vector
        def _(dve):
            whole(dve, dve_part)

        @block.tensor
        def _(pe):
            whole(pe, pe_part)


_INS = ['x', 'L0_conv_Wp', 'L0_conv_bp', 'L0_conv_Wo', 'L0_conv_bo', 'L1_conv_norm_w', 'L1_conv_norm_b',
        'L1_conv_qkv_w', 'L1_conv_proj_w', 'L1_conv_proj_b']
_OUTS = [((B, C, 32, 32), 'float32')]


def kernel(**inputs):
    import numpy as _np
    import concourse.bacc as _bacc
    from concourse import mybir as _mybir
    from concourse.bass_utils import run_bass_kernel_spmd as _run

    nc = _bacc.Bacc("TRN2", target_bir_lowering=False, num_devices=1)
    arrays, args = {}, []
    for name in _INS:
        a = _np.ascontiguousarray(inputs[name])
        arrays[f"in_{name}_dram"] = a
        args.append(nc.dram_tensor(f"in_{name}_dram", a.shape, _mybir.dt.from_np(a.dtype), kind="ExternalInput").ap())
    for i, (shape, dtype) in enumerate(_OUTS):
        dt = _mybir.dt.from_np(_np.dtype(dtype))
        args.append(nc.dram_tensor(f"out_{i}_dram", shape, dt, kind="ExternalOutput").ap())
    build_program(nc, *args)
    r = _run(nc, [arrays], core_ids=[0])
    got = tuple(r.results[0][f"out_{i}_dram"] for i in range(len(_OUTS)))
    return got[0]
```
